# Optimizing a Trainium2 kernel written in Bass

```python
import numpy as np
import jax
import jax.numpy as jnp

def _softmax(x, axis=-1):
    return jax.nn.softmax(x, axis=axis)

def _gelu(x):
    return jax.nn.gelu(x, approximate=True)

def _silu(x):
    return jax.nn.silu(x)

def _sigmoid(x):
    return jax.nn.sigmoid(x)

def _layernorm(x, axis=-1, eps=1e-05):
    m = jnp.mean(x, axis=axis, keepdims=True)
    v = jnp.var(x, axis=axis, keepdims=True)
    return (x - m) / jnp.sqrt(v + eps)

def _scatter_add(tgt, idx, src, axis=0):
    return tgt.at[idx].add(src)

def _segment_sum(src, seg, n):
    return jax.ops.segment_sum(src, seg, n)
kernel_name = 'mk_gnn_ffn_d1_gnn_r64_5c7ece'

def setup_inputs(seed: int=0):
    np.random.seed(seed)
    _w = jnp.asarray

    def _rec_inputs():
        import jax
        import jax.numpy as jnp
        _gk = jax.random.key(seed)
        x = -8.776e-05 + 1 * jax.random.normal(jax.random.fold_in(_gk, 1), (20000, 256), jnp.float32)
        src = jax.random.randint(jax.random.fold_in(_gk, 2), (10000,), 0, 20000, jnp.int32)
        dst = jax.random.randint(jax.random.fold_in(_gk, 3), (10000,), 0, 20000, jnp.int32)
        _o = jnp.argsort(dst, stable=True)
        src = src[_o]
        dst = dst[_o]
        edge_attr_3 = 0.00047201 + 1.00023 * jax.random.normal(jax.random.fold_in(_gk, 11), (10000, 3), jnp.float32)
        edge_attr_8 = jax.random.uniform(jax.random.fold_in(_gk, 12), (10000, 8), jnp.float32, 0.0, 0.999999)
        return (x, src, dst, edge_attr_3, edge_attr_8)
    x, src, dst, edge_attr_3, edge_attr_8 = _rec_inputs()

    def _L0_gnn_setup():
        import jax, jax.numpy as jnp
        import numpy as np
        MUL = 64
        NN = 20000
        NE = 5000
        NB = 8
        NH = 64
        NPATH = 5
        AVG_NEIGH = 16.0
        key = jax.random.key(seed)
        ks = jax.random.split(key, 8)
        return {'node_features': jax.random.normal(ks[0], (NN, 4 * MUL), jnp.float32), 'edge_vectors': jax.random.normal(ks[1], (NE, 3), jnp.float32), 'edge_lengths_embedding': jax.random.uniform(ks[2], (NE, NB), dtype=jnp.float32), 'fc_w1': jax.random.normal(ks[3], (NB, NH), jnp.float32), 'fc_w2': jax.random.normal(ks[4], (NH, NPATH * MUL), jnp.float32), 'lin_w0': jax.random.normal(ks[5], (MUL, MUL), jnp.float32), 'lin_w1': jax.random.normal(ks[6], (MUL, MUL), jnp.float32), 'edge_index': jax.random.randint(ks[7], (2, NE), 0, NN, dtype=jnp.int32)}
    _L0_gnn_all = _L0_gnn_setup()
    _L0_gnn_in = {k: v for k, v in _L0_gnn_all.items() if k in ('fc_w1', 'fc_w2', 'lin_w0', 'lin_w1')}
    del _L0_gnn_all

    def _L0_ffn_setup():
        import math
        import jax, jax.numpy as jnp
        import numpy as np
        CAPACITY_FACTOR = 1.25
        key = jax.random.key(seed)
        ks = jax.random.split(key, 5)
        B, L, D, F, E = (8, 128, 256, 1024, 8)
        h = jax.random.normal(ks[0], (B, L, D), dtype=jnp.float32)
        gate_w = jax.random.normal(ks[1], (D, E), dtype=jnp.float32) * 0.02
        gate_b = jnp.zeros((E,), dtype=jnp.float32)
        w1 = jax.random.normal(ks[2], (E, D, F), dtype=jnp.float32) * (1.0 / math.sqrt(D))
        b1 = jnp.zeros((E, F), dtype=jnp.float32)
        w2 = jax.random.normal(ks[3], (E, F, D), dtype=jnp.float32) * (1.0 / math.sqrt(F))
        b2 = jnp.zeros((E, D), dtype=jnp.float32)
        return {'h': h, 'gate_w': gate_w, 'gate_b': gate_b, 'w1': w1, 'b1': b1, 'w2': w2, 'b2': b2}
    _L0_ffn_all = _L0_ffn_setup()
    _L0_ffn_in = {k: v for k, v in _L0_ffn_all.items() if k in ('gate_w', 'gate_b', 'w1', 'b1', 'w2', 'b2')}
    del _L0_ffn_all
    return {'x': x, 'src': src, 'dst': dst, 'edge_attr_3': edge_attr_3, 'edge_attr_8': edge_attr_8, 'L0_gnn_fc_w1': _L0_gnn_in['fc_w1'], 'L0_gnn_fc_w2': _L0_gnn_in['fc_w2'], 'L0_gnn_lin_w0': _L0_gnn_in['lin_w0'], 'L0_gnn_lin_w1': _L0_gnn_in['lin_w1'], 'L0_ffn_gate_w': _L0_ffn_in['gate_w'], 'L0_ffn_gate_b': _L0_ffn_in['gate_b'], 'L0_ffn_w1': _L0_ffn_in['w1'], 'L0_ffn_b1': _L0_ffn_in['b1'], 'L0_ffn_w2': _L0_ffn_in['w2'], 'L0_ffn_b2': _L0_ffn_in['b2']}

def reference(x, src, dst, edge_attr_3, edge_attr_8, L0_gnn_fc_w1, L0_gnn_fc_w2, L0_gnn_lin_w0, L0_gnn_lin_w1, L0_ffn_gate_w, L0_ffn_gate_b, L0_ffn_w1, L0_ffn_b1, L0_ffn_w2, L0_ffn_b2):
    import jax
    import jax.numpy as jnp

    def _L0_gnn_ref(node_features, edge_vectors, edge_lengths_embedding, fc_w1, fc_w2, lin_w0, lin_w1, edge_index):
        import jax, jax.numpy as jnp
        import numpy as np
        MUL = 64
        NN = 20000
        NE = 5000
        NB = 8
        NH = 64
        NPATH = 5
        AVG_NEIGH = 16.0
        sender, receiver = (edge_index[0], edge_index[1])
        r = jnp.linalg.norm(edge_vectors, axis=-1, keepdims=True)
        sh1 = jnp.sqrt(jnp.asarray(3.0, edge_vectors.dtype)) * edge_vectors / (r + 1e-09)
        h = jax.nn.silu(edge_lengths_embedding @ fc_w1 / np.sqrt(NB))
        w = (h @ fc_w2 / np.sqrt(NH)).reshape(-1, NPATH, MUL)
        s = node_features[:, :MUL][sender]
        v = node_features[:, MUL:].reshape(-1, MUL, 3)[sender]
        dot = jnp.einsum('eui,ei->eu', v, sh1)
        crs = jnp.cross(v, sh1[:, None, :])
        inv_sqrt2 = 1.0 / np.sqrt(2.0)
        inv_sqrt3 = 1.0 / np.sqrt(3.0)
        m0 = (w[:, 0] * s + w[:, 3] * dot * inv_sqrt3) * inv_sqrt2
        m1 = (w[:, 1, :, None] * s[:, :, None] * sh1[:, None, :] + w[:, 2, :, None] * v + w[:, 4, :, None] * crs * inv_sqrt2) * inv_sqrt3
        agg0 = jax.ops.segment_sum(m0, receiver, num_segments=NN) / AVG_NEIGH
        agg1 = jax.ops.segment_sum(m1.reshape(-1, MUL * 3), receiver, num_segments=NN).reshape(-1, MUL, 3) / AVG_NEIGH
        out0 = agg0 @ lin_w0 / np.sqrt(MUL)
        out1 = jnp.einsum('nui,uv->nvi', agg1, lin_w1) / np.sqrt(MUL)
        upd = jnp.concatenate([out0, out1.reshape(-1, MUL * 3)], axis=-1)
        return upd + node_features

    def _L0_ffn_ref(h, gate_w, gate_b, w1, b1, w2, b2):
        import math
        import jax, jax.numpy as jnp
        import numpy as np
        CAPACITY_FACTOR = 1.25
        B, L, D = h.shape
        E = gate_w.shape[1]
        T = B * L
        C = max(1, math.ceil(CAPACITY_FACTOR * T / E))
        x = h.reshape(T, D)
        logits = x @ gate_w + gate_b
        probs = jax.nn.softmax(logits, axis=-1)
        idx = jnp.argmax(probs, axis=-1)
        prb = jnp.take_along_axis(probs, idx[:, None], axis=1)[:, 0]
        one_hot = jax.nn.one_hot(idx, E, dtype=jnp.float32)
        pos = (jnp.cumsum(one_hot, axis=0) * one_hot).sum(-1).astype(jnp.int32) - 1
        kept = pos < C
        pos_safe = jnp.where(kept, pos, C)
        buf = jnp.zeros((E, C, D), dtype=h.dtype).at[idx, pos_safe].set(x, mode='drop')
        hmid = jax.nn.relu(jnp.einsum('ecd,edf->ecf', buf, w1) + b1[:, None, :])
        ybuf = jnp.einsum('ecf,efd->ecd', hmid, w2) + b2[:, None, :]
        pos_g = jnp.minimum(pos, C - 1)
        y_tok = ybuf[idx, pos_g] * (prb * kept)[:, None]
        y = y_tok.reshape(B, L, D)
        y = jnp.nan_to_num(y, nan=0.0, posinf=10000.0, neginf=-10000.0)
        return y
    edge_index = jnp.stack([src, dst])
    x = x + _L0_gnn_ref(_layernorm(x, axis=-1), edge_attr_3, edge_attr_8, L0_gnn_fc_w1, L0_gnn_fc_w2, L0_gnn_lin_w0, L0_gnn_lin_w1, edge_index)
    x = x + _L0_ffn_ref(_layernorm(x, axis=-1)[None], L0_ffn_gate_w, L0_ffn_gate_b, L0_ffn_w1, L0_ffn_b1, L0_ffn_w2, L0_ffn_b2)[0]
    return x

_drawn_inputs = setup_inputs


def setup_inputs(seed=0):
    import zlib

    import numpy as np

    out = dict(_drawn_inputs(seed))
    spreads = {'L0_ffn_gate_b': (0.0, 0.8), 'L0_ffn_b1': (0.0, 2.0), 'L0_ffn_b2': (0.0, 2.0)}
    factors = {'edge_attr_3': 8.0,
     'edge_attr_8': 8.0,
     'L0_gnn_fc_w1': 7.344,
     'L0_gnn_fc_w2': 7.204,
     'L0_gnn_lin_w0': 8.0,
     'L0_gnn_lin_w1': 7.767,
     'L0_ffn_gate_w': 8.0,
     'L0_ffn_w1': 8.0,
     'L0_ffn_w2': 8.0}
    for name, (base, spread) in spreads.items():
        noise = np.random.default_rng([zlib.crc32(name.encode()), seed]).standard_normal(out[name].shape)
        drawn = base * np.exp(spread * noise) if base else spread * noise
        out[name] = jnp.asarray(drawn.astype(out[name].dtype))
    for name, factor in factors.items():
        out[name] = (out[name] * factor).astype(out[name].dtype)
    return out
```

```python
from contextlib import ExitStack

import numpy as np

import concourse.bass as bass
from concourse import mybir

ALU = mybir.AluOpType
ACT = mybir.ActivationFunctionType
AX = mybir.AxisListType
F32 = mybir.dt.float32
F32R = mybir.dt.float32r
BF16 = mybir.dt.bfloat16
I32 = mybir.dt.int32
U32 = mybir.dt.uint32

P = 128
D = 256
MUL = 64
NN, NE = 20000, 10000
GT = 4
GR = GT * P
NG = -(-NN // GR)
NT = NG * GT
ROWS = NG * GR
EG = -(-NE // GR)
EPAD = (EG + 2) * GR
NEXP, HID = 8, 1024
CAP = -(-5 * NN // (4 * NEXP))
BT = 5
BR = BT * P
EB = -(-CAP // BR)
NB = NEXP * EB
EST = EB * BT
NST = NEXP * EST
EPS = 1e-5
LARGEST = float(np.finfo(np.float32).max)
TABLES = 16 * 8
AHALF = NG // 4


class Chain:

    def __init__(self, engine, sem, spare=None):
        self.engine, self.sem, self.base, self.n, self.spare = engine, sem, 0, 0, spare

    def apart(self):
        self.engine.sem_inc(self.spare, 1)

    def mark(self, ins):
        ins.then_inc(self.sem, 1)
        self.n += 1
        return ins

    def wait(self, back=0):
        self.engine.wait_ge(self.sem, self.base + (self.n - back))

    def link(self, ins):
        self.mark(ins)
        self.wait()
        if self.spare is not None:
            self.apart()

    def enter(self, base):
        self.base, self.n = base, 0


def edge_and_node_block(nc, io, x1):
    assert NG % 4 == 0 and EG == 2 * AHALF and EG % 2 == 0
    with ExitStack() as ctx:
        def sb(name, shape, dt=F32):
            return ctx.enter_context(nc.sbuf_tensor(name, shape, dt))

        def ps(name, shape, dt=F32):
            return ctx.enter_context(nc.psum_tensor(name, shape, dt))

        def sem(name):
            return ctx.enter_context(nc.semaphore(name))

        src = sb("src", [P, EPAD // P], I32)
        dst_col = sb("dst_col", [P, EG * GT], I32)
        dst_f = sb("dst_f", [P, EG * GT])
        dst_less_trash = sb("dst_less_trash", [P, EG * GT])
        trash = sb("trash", [P, GT])
        edge_vec = sb("edge_vec", [P, EPAD // P, 3])
        edge_sq = sb("edge_sq", [P, EPAD // P, 3])
        edge_len = sb("edge_len", [P, EPAD // P])
        half = sb("half", [P, EPAD // P])
        minus_half = sb("minus_half", [P, 16])
        edge_dir = sb("edge_dir", [P, EPAD // P, 4])
        upper = sb("upper", [P, GR])
        lin = sb("lin", [P, 2, D])
        fc1 = sb("fc1", [8, MUL])
        fc2 = sb("fc2", [MUL, 5 * MUL])
        src_now = [sb(f"src_now{h}", [P, GT], I32) for h in range(2)]
        row_now = [sb(f"row_now{h}", [P, GT], I32) for h in range(2)]
        upd_now = [sb(f"upd_now{h}", [P, GT, D]) for h in range(2)]
        xin = sb("xin", [P, 4, GT, D])
        node_stats = sb("node_stats", [P, 4 * GT, 6])
        node_mv = sb("node_mv", [P, 4 * GT, 2])
        node_var = sb("node_var", [P, 4 * GT])
        node_rstd = sb("node_rstd", [P, 4 * GT])
        node_minus_rstd = sb("node_minus_rstd", [P, 4 * GT])
        node_scale = sb("node_scale", [P, 4 * GT])
        node_bias = sb("node_bias", [P, 4 * GT])
        xe = [sb(f"xe{h}", [P, GT, D]) for h in range(2)]
        edge_stats = sb("edge_stats", [P, GT, 6])
        edge_mv = sb("edge_mv", [P, GT, 2])
        edge_var = sb("edge_var", [P, GT])
        edge_rstd = sb("edge_rstd", [P, GT])
        edge_minus_rstd = sb("edge_minus_rstd", [P, GT])
        edge_shift = sb("edge_shift", [P, GT])
        coef_scale = [sb(f"coef_scale{h}", [P, GT, 4]) for h in range(2)]
        coef_bias = [sb(f"coef_bias{h}", [P, GT, 4]) for h in range(2)]
        y = [sb(f"y{h}", [P, GT, 4, D]) for h in range(2)]
        dst_row = [sb(f"dst_row{h}", [P, GR], I32) for h in range(2)]
        emb = [sb(f"emb{h}", [8, GR]) for h in range(2)]
        hidden = sb("hidden", [MUL, GR])
        same = sb("same", [P, GT, GR])
        later = sb("later", [P, GT])
        pick = sb("pick", [P, GT])
        msg = sb("msg", [P, GT, D])
        tmp_a = sb("tmp_a", [P, 2, 3 * MUL])
        tmp_b = sb("tmp_b", [P, 2, 3 * MUL])
        tmp_c = sb("tmp_c", [P, 2, 3 * MUL])
        tmp_d = sb("tmp_d", [P, 2, MUL])
        tmp_e = sb("tmp_e", [P, 2, MUL])
        tmp_f = sb("tmp_f", [P, 2, MUL])
        done = sb("done", [P, 1])
        tmp_g = sb("tmp_g", [P, 2, 3 * MUL])
        tmp_h = sb("tmp_h", [P, 2, 3 * MUL])
        agg = sb("agg", [P, 2, GR])
        upd = sb("upd", [P, EG * GT, D])
        upd_row = sb("upd_row", [P, EG * GT], I32)

        ps_w = ps("ps_w", [P, GT, 512])
        ps_h = ps("ps_h", [MUL, GR])
        ps_agg = ps("ps_agg", [P, 2, GR])
        ps_lin = ps("ps_lin", [P, 2, D])

        tables_in = sem("tables_in")
        x_in = [sem(f"x_in{a}") for a in range(4)]
        x1_out = [sem(f"x1_out{a}") for a in range(4)]
        dst_in = [sem(f"dst_in{h}") for h in range(2)]
        emb_in = [sem(f"emb_in{h}") for h in range(2)]
        gathered = [sem(f"gathered{h}") for h in range(2)]
        scattered = sem("scattered")
        dve_step = sem("dve_step")
        pool_step = sem("pool_step")
        pool_spare = sem("pool_spare")
        dve_spare = sem("dve_spare")
        node_mv_ready = sem("node_mv_ready")
        node_coef_ready = sem("node_coef_ready")
        act_rows_ready = sem("act_rows_ready")
        pool_rows_ready = sem("pool_rows_ready")
        len_ready = sem("len_ready")
        dir_ready = sem("dir_ready")
        weights_ready = sem("weights_ready")
        edge_mv_ready = sem("edge_mv_ready")
        coef_ready = sem("coef_ready")
        y0_ready = sem("y0_ready")
        y_ready = sem("y_ready")
        same_ready = sem("same_ready")
        msg_ready = sem("msg_ready")
        row_ready = sem("row_ready")
        ps_h_ready = sem("ps_h_ready")
        hidden_ready = sem("hidden_ready")
        ps_w_ready = sem("ps_w_ready")
        ps_agg_ready = sem("ps_agg_ready")
        agg_ready = sem("agg_ready")
        ps_lin_ready = sem("ps_lin_ready")
        upd_ready = sem("upd_ready")

        x_v = io["x"].rearrange("(g t p) c -> g p t c", t=GT, p=P)
        x1_v = x1.rearrange("(g t p) c -> g p t c", t=GT, p=P)
        dst_v = io["dst"].rearrange("(g c) -> g c", c=GR)

        block = ctx.enter_context(nc.Block())

        @block.sync
        def _(sp):
            def load_rows(group, a):
                sp.dma_start(xin[:, a], x_v[group]).then_inc(x_in[a], 16)

            def load_edges(q, h):
                sp.dma_start(emb[h][:], io["emb"][q]).then_inc(emb_in[h], 16)
                sp.dma_start(dst_row[h][:], dst_v[bass.ds(q, 1)].broadcast_to([P, GR])).then_inc(dst_in[h], 16)

            sp.dma_start(src[:], io["src_tiles"]).then_inc(tables_in, 16)
            sp.dma_start(dst_col[:], io["dst_tiles"]).then_inc(tables_in, 16)
            sp.dma_start(edge_vec[:], io["vec_tiles"]).then_inc(tables_in, 16)
            for a in range(4):
                load_rows(a, a)
            sp.dma_start(trash[:], io["trash"]).then_inc(tables_in, 16)
            sp.dma_start(upper[:], io["upper"]).then_inc(tables_in, 16)
            sp.dma_start(lin[:], io["lin"]).then_inc(tables_in, 16)
            sp.dma_start(fc1[:], io["fc1"]).then_inc(tables_in, 16)
            sp.dma_start(fc2[:], io["fc2"]).then_inc(tables_in, 16)
            load_edges(0, 0)
            load_edges(1, 1)

            def step(k, h, q, nodes):
                if nodes:
                    for a in range(4):
                        if a < 2:
                            sp.wait_ge(act_rows_ready, 2 * q + (a + 1))
                        else:
                            sp.wait_ge(pool_rows_ready, 2 * q + (a - 1))
                        sp.dma_start(x1_v[4 * q + a], xin[:, a]).then_inc(x1_out[a], 16)
                    for a in range(4):
                        sp.wait_ge(x1_out[a], 16 * q + 16)
                        load_rows(4 * q + (4 + a), a)
                sp.wait_ge(hidden_ready, q + 1)
                sp.wait_ge(same_ready, q + 1)
                load_edges(q + 2, h)

            with sp.Fori(0, AHALF // 2 - 1) as k:
                for h in range(2):
                    step(k, h, 2 * k + h, True)
            for h in range(2):
                q = AHALF - 2 + h
                for a in range(4):
                    if a < 2:
                        sp.wait_ge(act_rows_ready, 2 * q + a + 1)
                    else:
                        sp.wait_ge(pool_rows_ready, 2 * q + a - 1)
                    sp.dma_start(x1_v[4 * q + a], xin[:, a]).then_inc(x1_out[a], 16)
                if h == 0:
                    for a in range(4):
                        sp.wait_ge(x1_out[a], 16 * q + 16)
                        load_rows(4 * q + 4 + a, a)
                sp.wait_ge(hidden_ready, q + 1)
                sp.wait_ge(same_ready, q + 1)
                load_edges(q + 2, h)
            with sp.Fori(AHALF // 2, EG // 2) as k:
                for h in range(2):
                    step(k, h, 2 * k + h, False)
            for h in range(2):
                sp.wait_ge(emb_in[h], 16 * (EG // 2 + 1))
                sp.wait_ge(dst_in[h], 16 * (EG // 2 + 1))
            sp.wait_ge(scattered, 64 * (EG + 1))
            for a in range(4):
                sp.wait_ge(x1_out[a], 16 * AHALF)

        @block.gpsimd
        def _(pool):
            chain = Chain(pool, pool_step, pool_spare)

            def gather(q, h):
                chain.link(nc.gpsimd.tensor_copy(src_now[h][:], src[:, bass.ds(GT * q, GT)]))
                for t in range(GT):
                    nc.gpsimd.indirect_dma_start(
                        xe[h][:, t, :], None, io["x"],
                        bass.IndirectOffsetOnAxis(src_now[h][:, t:t + 1].bitcast(U32), 0),
                        bounds_check=NN - 1,
                    ).then_inc(gathered[h], 16)

            def affine_coefs(mv, var, rstd, minus_rstd, n):
                chain.link(nc.gpsimd.tensor_scalar(var[:], mv[:, :, 1], EPS, None, ALU.add))
                chain.link(nc.gpsimd.tensor_tensor(rstd[:], var[:], minus_half[:, :n], ALU.pow))
                chain.link(nc.gpsimd.tensor_scalar(minus_rstd[:], rstd[:], -1.0, None, ALU.mult))

            def edge_coefs(q, h):
                pool.wait_ge(edge_mv_ready, q + 1)
                chain.apart()
                affine_coefs(edge_mv, edge_var, edge_rstd, edge_minus_rstd, GT)
                chain.link(nc.gpsimd.tensor_tensor(edge_shift[:], edge_mv[:, :, 0], edge_minus_rstd[:], ALU.mult))
                direction = edge_dir[:, bass.ds(GT * q, GT), :]
                nc.gpsimd.tensor_tensor(coef_scale[h][:], direction,
                                        edge_rstd[:].unsqueeze(2).broadcast_to([P, GT, 4]), ALU.mult)
                nc.gpsimd.tensor_tensor(coef_bias[h][:], direction,
                                        edge_shift[:].unsqueeze(2).broadcast_to([P, GT, 4]),
                                        ALU.mult).then_inc(coef_ready, 1)

            def node_rows(q):
                pool.wait_ge(node_mv_ready, q + 1)
                chain.apart()
                affine_coefs(node_mv, node_var, node_rstd, node_minus_rstd, 4 * GT)
                chain.link(nc.gpsimd.tensor_scalar(node_scale[:], node_rstd[:], 1.0, None, ALU.add))
                nc.gpsimd.tensor_tensor(node_bias[:], node_mv[:, :, 0], node_minus_rstd[:],
                                        ALU.mult).then_inc(node_coef_ready, 1)
                pool.wait_ge(node_coef_ready, q + 2)
                chain.apart()
                for a in (2, 3):
                    for t in range(GT):
                        c = a * GT + t
                        ins = nc.gpsimd.tensor_scalar(xin[:, a, t], xin[:, a, t], node_scale[:, c:c + 1],
                                                      node_bias[:, c:c + 1], ALU.mult, ALU.add)
                    ins.then_inc(pool_rows_ready, 1)

            def scatter(g, h):
                pool.wait_ge(upd_ready, 2 * g + 3)
                pool.wait_ge(row_ready, g + 1)
                chain.apart()
                chain.mark(nc.gpsimd.tensor_copy(row_now[h][:], upd_row[:, bass.ds(GT * g, GT)]))
                chain.link(nc.gpsimd.tensor_copy(upd_now[h][:], upd[:, bass.ds(GT * g, GT), :]))
                pool.wait_ge(scattered, 64 * g + 64)
                chain.apart()
                for t in range(GT):
                    nc.gpsimd.indirect_dma_start(
                        x1, bass.IndirectOffsetOnAxis(row_now[h][:, t:t + 1].bitcast(U32), 0),
                        upd_now[h][:, t, :], None, bounds_check=ROWS + GR - 1, compute_op=ALU.add,
                    ).then_inc(scattered, 16)

            def read_ahead(q, h):
                pool.wait_ge(y_ready, q - 1)
                pool.wait_ge(y0_ready, q - 1)
                chain.apart()
                gather(q, h)

            nc.gpsimd.memset(half[:], 0.5)
            nc.gpsimd.memset(minus_half[:], -0.5)
            chain.mark(nc.gpsimd.memset(y[1][:], 0.0))
            pool.wait_ge(pool_step, 1)
            for t in range(GT):
                pool.dma_start(x1_v[NG, :, t], y[1][:, t, 0, :]).then_inc(scattered, 16)
            pool.wait_ge(tables_in, TABLES)
            gather(0, 0)
            gather(1, 1)
            pool.wait_ge(dve_step, 2)
            nc.gpsimd.tensor_tensor(edge_len[:], edge_len[:], half[:], ALU.pow).then_inc(len_ready, 1)
            pool.wait_ge(dir_ready, 1)
            edge_coefs(0, 0)

            def step(k, h, nodes):
                q = 2 * k + h
                if nodes:
                    node_rows(q)
                edge_coefs(q + 1, 1 - h)
                read_ahead(q + 2, h)

            first = chain.n
            per = 4 + 4 + 1
            with pool.Fori(0, AHALF // 2) as k:
                for h in range(2):
                    chain.enter(first + (2 * k + h) * per)
                    step(k, h, True)
                    assert chain.n == per, chain.n
            first += AHALF * per
            for a in range(4):
                pool.wait_ge(x1_out[a], 16 * AHALF)
            per = 4 + 1 + 4
            with pool.Fori(AHALF // 2, EG // 2) as k:
                for h in range(2):
                    chain.enter(first + (2 * k + h - AHALF) * per)
                    step(k, h, False)
                    for s in range(2):
                        scatter(2 * (2 * k + h - AHALF) + s, s)
                    assert chain.n == per, chain.n
            pool.wait_ge(scattered, 64 * (EG + 1))
            for h in range(2):
                pool.wait_ge(gathered[h], 64 * (EG // 2 + 1))

        @block.scalar
        def _(act):
            def rows_times_direction(q, h):
                act.wait_ge(coef_ready, q + 1)
                for t in range(GT):
                    for j in range(1, 4):
                        ins = nc.scalar.activation(y[h][:, t, j, :], xe[h][:, t, :], ACT.Identity,
                                                   bias=coef_bias[h][:, t, j:j + 1],
                                                   scale=coef_scale[h][:, t, j:j + 1])
                ins.then_inc(y_ready, 1)

            def radial_hidden(q):
                act.wait_ge(ps_h_ready, q + 1)
                nc.scalar.activation(hidden[:], ps_h[:], ACT.Silu, scale=8 ** -0.5).then_inc(hidden_ready, 1)

            rows_times_direction(0, 0)
            radial_hidden(0)

            def step(k, h, nodes):
                q = 2 * k + h
                if nodes:
                    act.wait_ge(node_coef_ready, q + 2)
                    for a in range(2):
                        for t in range(GT):
                            c = a * GT + t
                            ins = nc.scalar.activation(xin[:, a, t], xin[:, a, t], ACT.Identity,
                                                       bias=node_bias[:, c:c + 1],
                                                       scale=node_scale[:, c:c + 1])
                        ins.then_inc(act_rows_ready, 1)
                act.wait_ge(msg_ready, q + 1)
                rows_times_direction(q + 1, 1 - h)
                act.wait_ge(ps_w_ready, q + 1)
                radial_hidden(q + 1)
                act.wait_ge(ps_agg_ready, q + 2)
                nc.scalar.copy(agg[:, 0], ps_agg[:, 0])
                nc.scalar.copy(agg[:, 1], ps_agg[:, 1]).then_inc(agg_ready, 1)
                for s in range(2):
                    act.wait_ge(ps_lin_ready, 2 * q + (s + 1))
                    nc.scalar.copy(upd[:, bass.ds(GT * q + 2 * s, 2), :], ps_lin[:]).then_inc(upd_ready, 1)

            act.wait_ge(scattered, 64)
            with act.Fori(0, AHALF // 2) as k:
                for h in range(2):
                    step(k, h, True)
            with act.Fori(AHALF // 2, EG // 2) as k:
                for h in range(2):
                    step(k, h, False)

        @block.tensor
        def _(pe):
            def radial_first(q, k, h):
                pe.wait_ge(emb_in[h], 16 * k + 16)
                nc.tensor.matmul(ps_h[:], fc1[:], emb[h][:], start=True, stop=True).then_inc(ps_h_ready, 1)

            pe.wait_ge(tables_in, TABLES)
            radial_first(0, 0, 0)
            pe.wait_ge(weights_ready, 1)

            def step(k, h):
                q = 2 * k + h
                pe.wait_ge(hidden_ready, q + 1)
                pe.wait_ge(msg_ready, q + 1)
                for t in range(GT):
                    ins = nc.tensor.matmul(ps_w[:, t, :5 * MUL], hidden[:, t * P:(t + 1) * P], fc2[:],
                                           start=True, stop=True)
                ins.then_inc(ps_w_ready, 1)
                radial_first(q + 1, k + h, 1 - h)
                pe.wait_ge(same_ready, q + 1)
                pe.wait_ge(msg_ready, q + 2)
                pe.wait_ge(agg_ready, q + 1)
                for c in range(2):
                    for t in range(GT):
                        ins = nc.tensor.matmul(ps_agg[:, c, t * P:], msg[:, t, c * P:(c + 1) * P],
                                               same[:, t, :GR - t * P], start=t == 0, stop=t == GT - 1)
                ins.then_inc(ps_agg_ready, 1)
                pe.wait_ge(agg_ready, q + 2)
                for s in range(2):
                    pe.wait_ge(upd_ready, 2 * q + (s + 1))
                    for t in (2 * s, 2 * s + 1):
                        for c in range(2):
                            ins = nc.tensor.matmul(ps_lin[:, t % 2], agg[:, c, t * P:(t + 1) * P], lin[:, c],
                                                   start=c == 0, stop=c == 1)
                    ins.then_inc(ps_lin_ready, 1)

            with pe.Fori(0, EG // 2) as k:
                for h in range(2):
                    step(k, h)

        @block.vector
        def _(v):
            chain = Chain(v, dve_step, dve_spare)

            def node_statistics(q):
                for a in range(4):
                    v.wait_ge(x_in[a], 16 * q + 16)
                    for t in range(GT):
                        ins = nc.vector.bn_stats(node_stats[:, a * GT + t], xin[:, a, t])
                chain.link(ins)
                v.wait_ge(node_coef_ready, q + 1)
                chain.apart()
                for c in range(4 * GT):
                    ins = nc.vector.bn_aggr(node_mv[:, c], node_stats[:, c])
                ins.then_inc(node_mv_ready, 1)

            def edge_statistics(q, k, h):
                v.wait_ge(gathered[h], 64 * k + 64)
                for t in range(GT):
                    ins = nc.vector.bn_stats(edge_stats[:, t], xe[h][:, t])
                chain.link(ins)
                for t in range(GT):
                    ins = nc.vector.bn_aggr(edge_mv[:, t], edge_stats[:, t])
                ins.then_inc(edge_mv_ready, 1)

            def rows(q, h):
                v.wait_ge(coef_ready, q + 1)
                for t in range(GT):
                    ins = nc.vector.tensor_scalar(y[h][:, t, 0], xe[h][:, t], coef_scale[h][:, t, 0:1],
                                                  coef_bias[h][:, t, 0:1], ALU.mult, ALU.add)
                ins.then_inc(y0_ready, 1)

            def receivers(q, k, h):
                v.wait_ge(dst_in[h], 16 * k + 16)
                v.wait_ge(ps_agg_ready, q + 1)
                for t in range(GT):
                    ins = nc.vector.scalar_tensor_tensor(
                        out=same[:, t, :GR - t * P], in0=dst_row[h][:, t * P:],
                        scalar=dst_f[:, bass.ds(GT * q + t, 1)], in1=upper[:, :GR - t * P],
                        op0=ALU.is_equal, op1=ALU.mult, accum_out=later[:, t:t + 1])
                ins.then_inc(same_ready, 1)
                v.wait_ge(same_ready, q + 1)
                chain.link(nc.vector.scalar_tensor_tensor(
                    out=pick[:], in0=later[:], scalar=1.0, in1=dst_less_trash[:, bass.ds(GT * q, GT)],
                    op0=ALU.is_equal, op1=ALU.mult))
                nc.vector.tensor_tensor(upd_row[:, bass.ds(GT * q, GT)], pick[:], trash[:],
                                        ALU.add).then_inc(row_ready, 1)

            def messages(q, h):
                v.wait_ge(y0_ready, q + 1)
                v.wait_ge(y_ready, q + 1)
                v.wait_ge(ps_w_ready, q + 1)
                for s in range(2):
                    ts = slice(2 * s, 2 * s + 2)
                    xs = y[h][:, ts, :, :MUL]
                    xv = y[h][:, ts, :, MUL:].rearrange("p t j (u i) -> p t j u i", i=3)

                    def vec(x):
                        return x[:].rearrange("p t (u i) -> p t u i", i=3)

                    def w(n):
                        return ps_w[:, ts, n * MUL:(n + 1) * MUL]

                    def w3(n):
                        return w(n).unsqueeze(3).broadcast_to([P, 2, MUL, 3])

                    tt = nc.vector.tensor_tensor
                    if s:
                        chain.wait()
                    chain.mark(tt(tmp_d[:], xv[:, :, 1, :, 0], xv[:, :, 2, :, 1], ALU.add))
                    chain.mark(tt(tmp_e[:], xs[:, :, 0], w(0), ALU.mult))
                    chain.mark(tt(vec(tmp_b), xv[:, :, 0], w3(2), ALU.mult))
                    chain.mark(tt(vec(tmp_c), xs[:, :, 1:4].rearrange("p t j u -> p t u j"), w3(1), ALU.mult))
                    chain.wait(3)
                    chain.mark(tt(tmp_f[:], tmp_d[:], xv[:, :, 3, :, 2], ALU.add))
                    for i in range(3):
                        a, b = (i + 1) % 3, (i + 2) % 3
                        chain.mark(tt(vec(tmp_a)[:, :, :, i], xv[:, :, b + 1, :, a], xv[:, :, a + 1, :, b],
                                      ALU.subtract))
                    chain.wait(3)
                    chain.mark(tt(tmp_d[:], tmp_f[:], w(3), ALU.mult))
                    chain.mark(tt(tmp_g[:], tmp_b[:], tmp_c[:], ALU.add))
                    chain.wait(2)
                    chain.mark(tt(vec(tmp_h), vec(tmp_a), w3(4), ALU.mult))
                    chain.wait(2)
                    chain.mark(tt(msg[:, ts, :MUL], tmp_e[:], tmp_d[:], ALU.add))
                    chain.wait(1)
                    chain.mark(tt(msg[:, ts, MUL:], tmp_g[:], tmp_h[:], ALU.add))
                chain.wait()
                nc.vector.memset(done[:], 0.0).then_inc(msg_ready, 1)

            v.wait_ge(tables_in, TABLES)
            chain.link(nc.vector.tensor_tensor(edge_sq[:], edge_vec[:], edge_vec[:], ALU.mult))
            chain.link(nc.vector.tensor_reduce(edge_len[:], edge_sq[:], AX.X, ALU.add))
            nc.vector.tensor_copy(dst_f[:], dst_col[:]).then_inc(msg_ready, 1)
            nc.vector.tensor_scalar(lin[:], lin[:], 1 / (16 * 8), None, ALU.mult).then_inc(agg_ready, 1)
            for n, c in enumerate((2 ** -0.5, 3 ** -0.5, 3 ** -0.5, 6 ** -0.5, 6 ** -0.5)):
                ins = nc.vector.tensor_scalar(fc2[:, n * MUL:(n + 1) * MUL], fc2[:, n * MUL:(n + 1) * MUL],
                                              c / 8, None, ALU.mult)
            ins.then_inc(weights_ready, 1)
            v.wait_ge(msg_ready, 1)
            chain.link(nc.vector.tensor_tensor(
                dst_less_trash[:].rearrange("p (g t) -> p g t", t=GT),
                dst_f[:].rearrange("p (g t) -> p g t", t=GT),
                trash[:].unsqueeze(1).broadcast_to([P, EG, GT]), ALU.subtract))
            v.wait_ge(len_ready, 1)
            chain.link(nc.vector.tensor_scalar(edge_len[:], edge_len[:], 1e-9, None, ALU.add))
            chain.link(nc.vector.reciprocal(edge_len[:], edge_len[:]))
            chain.link(nc.vector.tensor_scalar(edge_vec[:], edge_vec[:], 3 ** 0.5, None, ALU.mult))
            nc.vector.memset(edge_dir[:, :, 0:1], 1.0).then_inc(ps_agg_ready, 1)
            nc.vector.tensor_tensor(edge_dir[:, :, 1:4], edge_vec[:],
                                    edge_len[:].unsqueeze(2).broadcast_to([P, EPAD // P, 3]),
                                    ALU.mult).then_inc(dir_ready, 1)
            nc.vector.memset(tmp_g[:], 0.0).then_inc(node_coef_ready, 1)
            nc.vector.memset(tmp_h[:], 0.0).then_inc(upd_ready, 1)
            edge_statistics(0, 0, 0)
            rows(0, 0)
            v.wait_ge(scattered, 64)

            def step(k, h, nodes):
                q = 2 * k + h
                if nodes:
                    node_statistics(q)
                edge_statistics(q + 1, k + h, 1 - h)
                receivers(q, k, h)
                rows(q + 1, 1 - h)
                messages(q, h)

            first = chain.n
            per = 3 + 2 * 13
            with v.Fori(0, AHALF // 2) as k:
                for h in range(2):
                    chain.enter(first + (2 * k + h) * per)
                    step(k, h, True)
                    assert chain.n == per, chain.n
            first += AHALF * per
            per -= 1
            with v.Fori(AHALF // 2, EG // 2) as k:
                for h in range(2):
                    chain.enter(first + (2 * k + h - AHALF) * per)
                    step(k, h, False)
                    assert chain.n == per, chain.n


def routing_block(nc, io, x1, take_row, put_row, first_block):
    U = 4
    with ExitStack() as ctx:
        def sb(name, shape, dt=F32):
            return ctx.enter_context(nc.sbuf_tensor(name, shape, dt))

        def ps(name, shape, dt=F32):
            return ctx.enter_context(nc.psum_tensor(name, shape, dt))

        def sem(name):
            return ctx.enter_context(nc.semaphore(name))

        rows = sb("rows", [P, U, GT, D])
        stats = [sb(f"stats{h}", [P, GT, 6]) for h in range(2)]
        mv = [sb(f"mv{h}", [P, GT, 2]) for h in range(2)]
        var = sb("var", [P, GT])
        rstd = [sb(f"rstd{a}", [P, GT]) for a in range(U)]
        minus_rstd = sb("minus_rstd", [P, GT])
        shift = [sb(f"shift{a}", [P, GT]) for a in range(U)]
        power = sb("power", [P, GT])
        xn = [sb(f"xn{h}", [P, GT, D]) for h in range(2)]
        xt = [sb(f"xt{h}", [P, 2, GR]) for h in range(2)]
        ident = sb("r_ident", [P, P])
        gate_w = sb("gate_w", [P, 2, NEXP])
        gate_b = sb("gate_b", [P, NEXP])
        logits = sb("logits", [P, NT, NEXP])
        valid = sb("valid", [P, NT])
        tile_no = sb("tile_no", [P, NT])
        row_no = sb("row_no", [P, 1])
        falling = sb("falling", [P, NEXP])
        thresholds = sb("thresholds", [P, EB])
        before_f = sb("before_f", [P, P])
        before = sb("before", [P, P], BF16)
        ones = sb("ones", [P, P], BF16)
        ones_row = sb("ones_row", [P, NT])
        iota_f = sb("iota_f", [P, 256])
        iota = sb("iota", [P, 256], BF16)
        best = sb("best", [P, NT])
        score = sb("score", [P, NT, NEXP])
        score2 = sb("score2", [P, NT, NEXP])
        first = sb("first", [P, NT])
        chosen = sb("chosen", [P, NEXP, NT], BF16)
        total = sb("total", [P, NEXP, NT])
        upto = sb("upto", [P, NEXP, NT])
        place = sb("place", [P, NEXP, NT])
        rank = sb("rank", [P, NT])
        rank_i = sb("rank_i", [P, NT], I32)
        high_i = sb("high_i", [P, NT], I32)
        low_i = sb("low_i", [P, NT], I32)
        high = sb("high", [P, NT])
        low = sb("low", [P, NT])
        upto_end = sb("upto_end", [P, NEXP])
        more = sb("more", [P, NEXP, EB])
        blocks_sum = sb("blocks_sum", [P, NEXP])
        blocks = sb("blocks", [P, NEXP])
        last_block = sb("last_block", [P, NEXP])
        begin = sb("begin", [P, NEXP])
        begin_tile = sb("begin_tile", [P, NT])
        kept = sb("kept", [P, NT])
        slot_tile = sb("slot_tile", [P, NT])
        slot_row = sb("slot_row", [P, NT])
        in_row = sb("in_row", [P, U, P], BF16)
        slot_rows = sb("slot_rows", [P, U])
        in_tile = sb("in_tile", [P, U, 2, NST], BF16)
        table = sb("table", [P, 2, NST])
        token = sb("token", [P, NST])
        empty = sb("empty", [P, NST])

        zeros = sb("zeros", [P, 2 * NST], BF16)
        banks = ps("banks", [P, 8, 512])
        ps_t = [banks[:, 2 * h:2 * h + 2] for h in range(2)]
        ps_l = [banks[:, 4 + h] for h in range(2)]
        ps_place = banks[:, 0:3].rearrange("p b c -> p (b c)")
        ps_total = banks[:, 3:6].rearrange("p b c -> p (b c)")
        ps_table = banks[:, 6]

        consts_in = sem("consts_in")
        rows_in = [sem(f"rows_in{a}") for a in range(U)]
        step_dve = sem("step_dve")
        spare_dve = sem("spare_dve")
        step_pool = sem("step_pool")
        spare_pool = sem("spare_pool")
        mv_ready = sem("mv_ready")
        coef_ready = sem("r_coef_ready")
        xn_ready = sem("xn_ready")
        turned = sem("turned")
        xt_act = sem("xt_act")
        xt_dve = sem("xt_dve")
        logits_ready = sem("logits_ready")
        logits_taken = sem("logits_taken")
        chosen_ready = sem("chosen_ready")
        before_ready = sem("before_ready")
        ones_ready = sem("ones_ready")
        total_ready = sem("total_ready")
        slots_ready = sem("slots_ready")
        in_row_ready = sem("in_row_ready")
        in_tile_ready = sem("in_tile_ready")
        table_step = sem("table_step")

        x1_v = x1[:ROWS].rearrange("(g t p) c -> g p t c", t=GT, p=P)
        KC = NG // U
        CONSTS = 16 * 11

        block = ctx.enter_context(nc.Block())

        @block.sync
        def _(sp):
            for a in range(U):
                sp.dma_start(rows[:, a], x1_v[a]).then_inc(rows_in[a], 16)
            for tile, name in ((ident, "ident"), (gate_w, "gate_w"), (gate_b, "gate_b"), (valid, "valid"),
                               (tile_no, "tile_no"), (row_no, "row_no"), (falling, "falling"),
                               (thresholds, "thresholds"), (before_f, "before"), (iota_f, "iota")):
                sp.dma_start(tile[:], io[name]).then_inc(consts_in, 16)
            sp.dma_start(ones_row[:], io["ones_row"]).then_inc(consts_in, 16)

            def step(k):
                for a in range(U):
                    sp.wait_ge(xn_ready, U * k + (a + 1))
                    sp.dma_start(rows[:, a], x1_v[U * k + (U + a)]).then_inc(rows_in[a], 16)

            with sp.Fori(0, KC - 1) as k:
                step(k)

        @block.gpsimd
        def _(pool):
            chain = Chain(pool, step_pool, spare_pool)

            def coefs(g, a):
                pool.wait_ge(mv_ready, g + 1)
                chain.apart()
                chain.link(nc.gpsimd.tensor_scalar(var[:], mv[a % 2][:, :, 1], EPS, None, ALU.add))
                chain.link(nc.gpsimd.tensor_tensor(rstd[a][:], var[:], power[:], ALU.pow))
                chain.link(nc.gpsimd.tensor_scalar(minus_rstd[:], rstd[a][:], -1.0, None, ALU.mult))
                nc.gpsimd.tensor_tensor(shift[a][:], mv[a % 2][:, :, 0], minus_rstd[:],
                                        ALU.mult).then_inc(coef_ready, 1)

            chain.link(nc.gpsimd.memset(power[:], -0.5))
            nc.gpsimd.memset(ones[:], 1.0).then_inc(ones_ready, 1)
            with pool.Fori(0, KC) as k:
                for a in range(U):
                    chain.enter(1 + (U * k + a) * 3)
                    coefs(U * k + a, a)
                    assert chain.n == 3
            pool.wait_ge(slots_ready, 1)
            pool.sem_inc(in_row_ready, 1)
            with pool.Fori(0, NT // U) as k:
                chain.enter(1 + 3 * NG + k)
                pool.wait_ge(in_row_ready, U * k + 1)
                chain.link(nc.gpsimd.tensor_copy(slot_rows[:], slot_row[:, bass.ds(U * k, U)]))
                for a in range(U):
                    pool.wait_ge(table_step, U * k + (a + 1))
                    chain.apart()
                    nc.gpsimd.tensor_scalar(in_row[:, a], iota[:, :P], slot_rows[:, a:a + 1], None,
                                            ALU.is_equal).then_inc(in_row_ready, 1)

        @block.scalar
        def _(act):
            def normalise(g, a):
                act.wait_ge(coef_ready, g + 1)
                for t in range(GT):
                    ins = nc.scalar.activation(xn[a % 2][:, t], rows[:, a, t], ACT.Identity,
                                               bias=shift[a][:, t:t + 1], scale=rstd[a][:, t:t + 1])
                ins.then_inc(xn_ready, 1)

            normalise(0, 0)

            def step(g, a, more):
                if more:
                    normalise(g + 1, (a + 1) % U)
                act.wait_ge(turned, g + 1)
                nc.scalar.copy(xt[a % 2][:, 0], ps_t[a % 2][:, 0]).then_inc(xt_act, 1)

            with act.Fori(0, KC - 1) as k:
                for a in range(U):
                    step(U * k + a, a, True)
            for a in range(U):
                step(U * (KC - 1) + a, a, a < U - 1)
            act.wait_ge(before_ready, 1)
            nc.scalar.copy(total[:].rearrange("p e t -> p (e t)"), ps_total[:, :NEXP * NT]).then_inc(total_ready, 1)

        @block.tensor
        def _(pe):
            pe.wait_ge(consts_in, CONSTS)

            def step(g, a):
                h = a % 2
                pe.wait_ge(xn_ready, g + 1)
                for c in range(2):
                    for t in range(GT):
                        ins = nc.tensor.transpose(ps_t[h][:, c, t * P:(t + 1) * P],
                                                  xn[h][:, t, c * P:(c + 1) * P], ident[:])
                ins.then_inc(turned, 1)
                pe.wait_ge(xt_act, g + 1)
                pe.wait_ge(xt_dve, g + 1)
                for t in range(GT):
                    for c in range(2):
                        ins = nc.tensor.matmul(ps_l[h][:, t * NEXP:(t + 1) * NEXP],
                                               xt[h][:, c, t * P:(t + 1) * P], gate_w[:, c],
                                               start=c == 0, stop=c == 1)
                ins.then_inc(logits_ready, 1)

            with pe.Fori(0, KC) as k:
                for a in range(U):
                    pe.wait_ge(logits_taken, U * k + (a + 1))
                    step(U * k + a, a)
            pe.wait_ge(ones_ready, 1)
            pe.wait_ge(chosen_ready, 1)
            flat = chosen[:].rearrange("p e t -> p (e t)")
            for weights, dest in ((before, ps_place), (ones, ps_total)):
                for c in range(0, NEXP * NT, 512):
                    w = min(512, NEXP * NT - c)
                    ins = nc.tensor.matmul(dest[:, c:c + w], weights[:], flat[:, c:c + w],
                                           start=True, stop=True)
            ins.then_inc(before_ready, 1)
            nc.tensor.matmul(ps_table[:, :2 * NST], zeros[:, :P], zeros[:], start=True,
                             stop=False).then_inc(table_step, U)
            with pe.Fori(0, NT // U) as k:
                for a in range(U):
                    pe.wait_ge(in_row_ready, U * k + (a + 2))
                    pe.wait_ge(in_tile_ready, U * k + (a + 1))
                    nc.tensor.matmul(ps_table[:, :2 * NST], in_row[:, a],
                                     in_tile[:, a].rearrange("p b c -> p (b c)"), start=False,
                                     stop=False).then_inc(table_step, 1)
            nc.tensor.matmul(ps_table[:, :2 * NST], zeros[:, :P], zeros[:], start=False,
                             stop=True).then_inc(table_step, 1)

        @block.vector
        def _(v):
            chain = Chain(v, step_dve, spare_dve)

            def statistics(g, k, a):
                v.wait_ge(rows_in[a], 16 * k + 16)
                for t in range(GT):
                    ins = nc.vector.bn_stats(stats[a % 2][:, t], rows[:, a, t])
                chain.link(ins)
                for t in range(GT):
                    ins = nc.vector.bn_aggr(mv[a % 2][:, t], stats[a % 2][:, t])
                ins.then_inc(mv_ready, 1)

            def take(g, h):
                v.wait_ge(turned, g + 1)
                nc.vector.tensor_copy(xt[h][:, 1], ps_t[h][:, 1]).then_inc(xt_dve, 1)
                v.wait_ge(logits_ready, g + 1)
                nc.vector.tensor_tensor(
                    logits[:, bass.ds(GT * g, GT), :],
                    ps_l[h][:, :GT * NEXP].rearrange("p (t e) -> p t e", e=NEXP),
                    gate_b[:].unsqueeze(1).broadcast_to([P, GT, NEXP]), ALU.add).then_inc(logits_taken, 1)

            v.wait_ge(consts_in, CONSTS)
            nc.vector.tensor_copy(before[:], before_f[:])
            nc.vector.tensor_copy(iota[:], iota_f[:])
            nc.vector.memset(zeros[:], 0.0).then_inc(logits_taken, 2)
            statistics(0, 0, 0)
            statistics(1, 0, 1)
            first_n = chain.n

            with v.Fori(0, KC - 1) as k:
                for a in range(U):
                    chain.enter(first_n + (U * k + a))
                    v.wait_ge(coef_ready, U * k + (a + 1))
                    statistics(U * k + (a + 2), k + (a + 2) // U, (a + 2) % U)
                    take(U * k + a, a % 2)
                    assert chain.n == 1
            chain.enter(first_n + U * (KC - 1))
            for a in range(U):
                g = U * (KC - 1) + a
                if a < U - 2:
                    statistics(g + 2, KC - 1, a + 2)
                take(g, a % 2)
            v.wait_ge(logits_taken, NG + 2)

            tt, ts, stt, red = (nc.vector.tensor_tensor, nc.vector.tensor_scalar,
                                nc.vector.scalar_tensor_tensor, nc.vector.tensor_reduce)

            def over_experts(x):
                return x[:].unsqueeze(2).broadcast_to([P, NT, NEXP])

            def over_tokens(x):
                return x[:].unsqueeze(1).broadcast_to([P, NT, NEXP])

            chain.link(red(best[:], logits[:], AX.X, ALU.max))
            chain.link(tt(score[:], logits[:], over_experts(best), ALU.is_equal))
            chain.link(tt(score2[:], score[:], over_tokens(falling), ALU.mult))
            chain.link(red(first[:], score2[:], AX.X, ALU.max))
            chain.link(tt(score[:], score2[:], over_experts(first), ALU.is_equal))
            tt(chosen[:].rearrange("p e t -> p t e"), score[:], over_experts(valid),
               ALU.mult).then_inc(chosen_ready, 1)
            v.wait_ge(total_ready, 1)
            for e in range(NEXP):
                ins = nc.vector.tensor_tensor_scan(upto[:, e], ones_row[:], total[:, e], 0.0, ALU.mult, ALU.add)
            chain.link(ins)
            chain.mark(nc.vector.tensor_copy(upto_end[:], upto[:, :, NT - 1]))
            chain.link(tt(place[:], upto[:], total[:], ALU.subtract))
            chain.link(tt(upto[:].rearrange("p e t -> p (e t)"), place[:].rearrange("p e t -> p (e t)"),
                          ps_place[:, :NEXP * NT], ALU.add))
            chain.link(tt(place[:], upto[:], chosen[:], ALU.mult))
            chain.link(red(rank[:], place[:].rearrange("p e t -> p t e"), AX.X, ALU.add))
            chain.link(tt(more[:], upto_end[:].unsqueeze(2).broadcast_to([P, NEXP, EB]),
                          thresholds[:].unsqueeze(1).broadcast_to([P, NEXP, EB]), ALU.is_gt))
            chain.link(red(blocks_sum[:], more[:], AX.X, ALU.add))
            chain.link(ts(blocks[:], blocks_sum[:], 1.0, None, ALU.max))
            chain.link(nc.vector.tensor_tensor_scan(last_block[:], ones_row[:, :NEXP], blocks[:], 0.0,
                                                    ALU.mult, ALU.add))
            chain.mark(nc.vector.tensor_copy(first_block[:, 1:], last_block[:1]))
            chain.mark(nc.vector.memset(first_block[:, :1], 0))
            chain.link(tt(begin[:], last_block[:], blocks[:], ALU.subtract))
            chain.link(tt(score2[:], chosen[:].rearrange("p e t -> p t e"), over_tokens(begin), ALU.mult))
            chain.link(red(begin_tile[:], score2[:], AX.X, ALU.add))
            chain.mark(nc.vector.tensor_copy(rank_i[:], rank[:]))
            chain.mark(stt(out=kept[:], in0=rank[:], scalar=float(CAP), in1=valid[:], op0=ALU.is_lt, op1=ALU.mult))
            chain.wait()
            chain.mark(ts(high_i[:], rank_i[:], 7, None, ALU.logical_shift_right))
            chain.mark(ts(low_i[:], rank_i[:], 127, None, ALU.bitwise_and))
            chain.wait()
            chain.mark(nc.vector.tensor_copy(high[:], high_i[:]))
            chain.mark(nc.vector.tensor_copy(low[:], low_i[:]))
            chain.wait()
            stt(out=slot_tile[:], in0=begin_tile[:], scalar=float(BT), in1=high[:], op0=ALU.mult, op1=ALU.add)
            chain.link(stt(out=slot_row[:], in0=kept[:], scalar=-1000.0, in1=low[:], op0=ALU.mult, op1=ALU.add))
            ts(slot_row[:], slot_row[:], 1000.0, None, ALU.add).then_inc(slots_ready, 1)
            v.wait_ge(slots_ready, 1)

            with v.Fori(0, NT // U) as k:
                for a in range(U):
                    v.wait_ge(table_step, U * k + (a + 1))
                    t = bass.ds(U * k + a, 1)
                    ts(in_tile[:, a, 0], iota[:, :NST], slot_tile[:, t], row_no[:], ALU.is_equal, ALU.mult)
                    ts(in_tile[:, a, 1], iota[:, :NST], slot_tile[:, t], tile_no[:, t], ALU.is_equal,
                       ALU.mult).then_inc(in_tile_ready, 1)
            v.wait_ge(table_step, U + NT + 1)
            chain.link(nc.vector.tensor_copy(table[:].rearrange("p b c -> p (b c)"), ps_table[:, :2 * NST]))
            chain.link(stt(out=token[:], in0=table[:, 1], scalar=float(P), in1=table[:, 0], op0=ALU.mult, op1=ALU.add))
            chain.mark(ts(empty[:], token[:], 0.0, float(ROWS), ALU.is_equal, ALU.mult))
            chain.mark(nc.vector.memset(take_row[:], ROWS - 1))
            chain.mark(nc.vector.memset(put_row[:], 1 << 17))
            chain.wait()
            chain.mark(stt(out=take_row[:, :NST], in0=token[:], scalar=-1.0, in1=empty[:], op0=ALU.add, op1=ALU.add))
            chain.link(ts(empty[:], empty[:], 8.0, None, ALU.mult))
            chain.link(stt(out=put_row[:, BT:], in0=token[:], scalar=-1.0, in1=empty[:], op0=ALU.add, op1=ALU.add))


def expert_block(nc, io, out, take_row, put_row, first_block):
    KF = HID // P
    HB = BR // 2
    W1 = 2 * HID
    WALL = W1 + KF * D
    with ExitStack() as ctx:
        def sb(name, shape, dt=F32):
            return ctx.enter_context(nc.sbuf_tensor(name, shape, dt))

        def ps(name, shape, dt=F32):
            return ctx.enter_context(nc.psum_tensor(name, shape, dt))

        def sem(name):
            return ctx.enter_context(nc.semaphore(name))

        raw = sb("raw", [P, WALL])
        w_hi = [sb(f"w_hi{s}", [P, WALL], F32R) for s in range(2)]
        w_lo = [sb(f"w_lo{s}", [P, WALL], F32R) for s in range(2)]
        b1 = sb("b1", [P, NEXP, KF])
        b2 = sb("b2", [P, NEXP, D])
        ident = sb("f_ident", [P, P])
        power = sb("f_power", [P, BT])
        gate_raw = sb("gate_raw", [P, 2 * NEXP])
        gate_parts = sb("gate_parts", [P, 2, 2, NEXP], F32R)
        gate_b = sb("f_gate_b", [P, NEXP])
        take_now = sb("take_now", [P, BT], I32)
        put_now = sb("put_now", [P, BT], I32)
        xg = sb("xg", [P, BT, D])
        stats = sb("f_stats", [P, BT, 6])
        mv = sb("f_mv", [P, BT, 2])
        var = sb("f_var", [P, BT])
        rstd = sb("f_rstd", [P, BT])
        minus_rstd = sb("f_minus_rstd", [P, BT])
        shift = sb("f_shift", [P, BT])
        xn = sb("f_xn", [P, BT, D])
        resid = sb("resid", [P, 3, BT, D])
        x_hi = sb("x_hi", [P, 2, BR], F32R)
        x_lo = sb("x_lo", [P, 2, BR], F32R)
        h_all = [sb(f"h_all{h}", [P, BR]) for h in range(2)]
        h_hi = sb("h_hi", [P, KF, BR], F32R)
        h_lo = sb("h_lo", [P, KF, BR], F32R)
        logit_parts = sb("logit_parts", [P, BT, 2 * NEXP])
        logits_sum = sb("logits_sum", [P, BT, NEXP])
        logits = sb("f_logits", [P, BT, NEXP])
        top = sb("top", [P, BT])
        below = sb("below", [P, BT, NEXP])
        power_e = sb("power_e", [P, BT, NEXP])
        total = sb("f_total", [P, BT])
        prob = sb("prob", [P, BT])
        y_sum = sb("y_sum", [P, 2, D])
        y_all = sb("y_all", [P, BT, D])
        finite = sb("finite", [P, BT, D], I32)
        negative = sb("negative", [P, BT, D])
        clean = sb("clean", [P, BT, D])
        y_out = sb("y_out", [P, BT, D])

        ps_h = ps("f_ps_h", [P, 2, 2, 512])
        ps_y = ps("f_ps_y", [P, 2, 512])
        ps_x = ps("f_ps_x", [P, 2, 512])

        consts_in = sem("f_consts_in")
        raw_in = [sem(f"raw_in{n}") for n in range(2)]
        gathered = sem("f_gathered")
        written = sem("written")
        step_dve = sem("f_step_dve")
        spare_dve = sem("f_spare_dve")
        step_pool = sem("f_step_pool")
        spare_pool = sem("f_spare_pool")
        gate_ready = sem("gate_ready")
        hi_ready = sem("hi_ready")
        lo_ready = sem("lo_ready")
        mv_ready = sem("f_mv_ready")
        coef_ready = sem("f_coef_ready")
        xn_ready = sem("f_xn_ready")
        resid_ready = sem("resid_ready")
        turned = sem("f_turned")
        x_hi_ready = sem("x_hi_ready")
        x_lo_ready = sem("x_lo_ready")
        logits_ready = sem("f_logits_ready")
        logits_taken = sem("f_logits_taken")
        below_ready = sem("below_ready")
        exp_ready = sem("exp_ready")
        prob_ready = sem("prob_ready")
        cleared = sem("cleared")
        h_ready = sem("h_ready")
        h_hi_ready = sem("h_hi_ready")
        h_lo_ready = sem("h_lo_ready")
        y_ready = sem("f_y_ready")
        y_sum_ready = sem("y_sum_ready")
        y_all_ready = sem("y_all_ready")
        clean_ready = sem("clean_ready")
        done_ready = sem("done_ready")

        w1_v = io["w1"].rearrange("e (k p) f -> e p k f", p=P)
        w2_v = io["w2"].rearrange("e (f p) c -> e p f c", p=P)
        CONSTS = 16 * 5

        def bounds(engine, e):
            return (engine.value_load(first_block[0:1, bass.ds(e, 1)], min_val=0, max_val=NB - 1),
                    engine.value_load(first_block[0:1, bass.ds(e + 1, 1)], min_val=1, max_val=NB))

        block = ctx.enter_context(nc.Block())

        @block.sync
        def _(sp):
            def load_weights(e):
                sp.dma_start(raw[:, :W1].rearrange("p (k f) -> p k f", k=2),
                             w1_v[e]).then_inc(raw_in[0], 16)
                sp.dma_start(raw[:, W1:].rearrange("p (f c) -> p f c", f=KF),
                             w2_v[e]).then_inc(raw_in[1], 16)

            load_weights(0)
            sp.dma_start(b1[:], io["b1"]).then_inc(consts_in, 16)
            sp.dma_start(b2[:].rearrange("p e c -> p (e c)"), io["b2"].broadcast_to([P, NEXP * D])).then_inc(consts_in, 16)
            sp.dma_start(ident[:], io["ident"]).then_inc(consts_in, 16)
            sp.dma_start(gate_raw[:].rearrange("p (k e) -> p k e", k=2), io["gate_w"]).then_inc(consts_in, 16)
            sp.dma_start(gate_b[:], io["gate_b"]).then_inc(consts_in, 16)
            sp.wait_ge(hi_ready, 1)
            sp.wait_ge(lo_ready, 1)
            load_weights(1)
            with sp.Fori(0, NEXP - 2) as e:
                sp.wait_ge(hi_ready, e + 2)
                sp.wait_ge(lo_ready, e + 2)
                load_weights(e + 2)
            sp.wait_ge(hi_ready, NEXP)
            sp.wait_ge(lo_ready, NEXP)
            load_weights(NEXP - 1)
            for n in range(2):
                sp.wait_ge(raw_in[n], 16 * (NEXP + 1))

        @block.gpsimd
        def _(pool):
            chain = Chain(pool, step_pool, spare_pool)

            def gather(b):
                chain.link(nc.gpsimd.tensor_copy(take_now[:], take_row[:, bass.ds(BT * b, BT)]))
                for i in range(BT):
                    nc.gpsimd.indirect_dma_start(
                        xg[:, i, :], None, out,
                        bass.IndirectOffsetOnAxis(take_now[:, i:i + 1].bitcast(U32), 0),
                        bounds_check=ROWS - 1).then_inc(gathered, 16)

            def coefs(b):
                pool.wait_ge(mv_ready, b + 1)
                chain.apart()
                chain.link(nc.gpsimd.tensor_scalar(var[:], mv[:, :, 1], EPS, None, ALU.add))
                chain.link(nc.gpsimd.tensor_tensor(rstd[:], var[:], power[:], ALU.pow))
                chain.link(nc.gpsimd.tensor_scalar(minus_rstd[:], rstd[:], -1.0, None, ALU.mult))
                nc.gpsimd.tensor_tensor(shift[:], mv[:, :, 0], minus_rstd[:], ALU.mult).then_inc(coef_ready, 1)

            def split_low(e, s):
                for n in range(2):
                    pool.wait_ge(raw_in[n], 16 * e + 16)
                pool.wait_ge(hi_ready, e + 1)
                chain.apart()
                nc.gpsimd.tensor_tensor(w_lo[s][:], raw[:], w_hi[s][:].bitcast(F32),
                                        ALU.subtract).then_inc(lo_ready, 1)

            def write(b):
                pool.wait_ge(clean_ready, b + 1)
                pool.wait_ge(written, 80 * b + 16)
                chain.apart()
                chain.mark(nc.gpsimd.tensor_copy(put_now[:], put_row[:, bass.ds(BT * b, BT)]))
                nc.gpsimd.tensor_tensor(y_out[:].unsqueeze(1), clean[:].unsqueeze(1),
                                        resid[:, bass.ds((b + 2) % 3, 1)], ALU.add).then_inc(done_ready, 1)
                pool.wait_ge(done_ready, b + 2)
                chain.wait()
                chain.apart()
                for i in range(BT):
                    nc.gpsimd.indirect_dma_start(
                        out, bass.IndirectOffsetOnAxis(put_now[:, i:i + 1].bitcast(U32), 0),
                        y_out[:, i, :], None, bounds_check=ROWS - 1, oob_is_err=False,
                    ).then_inc(written, 16)

            chain.link(nc.gpsimd.memset(power[:], -0.5))
            chain.mark(nc.gpsimd.memset(resid[:, 2], 0.0))
            chain.mark(nc.gpsimd.memset(y_out[:], 0.0))
            chain.link(nc.gpsimd.memset(y_all[:], 0.0))
            pool.sem_inc(cleared, 1)
            pool.dma_start(io["spare"], y_out[:, 0, :]).then_inc(written, 16)
            pool.sem_inc(done_ready, 1)
            gather(0)
            split_low(0, 0)
            coefs(0)
            pool.wait_ge(resid_ready, 1)
            gather(1)
            coefs(1)
            first = chain.n
            PER = 1 + 1 + 3
            with pool.Fori(0, NEXP // 2) as pair:
                for s in range(2):
                    e = 2 * pair + s
                    split_low(e + 1, 1 - s)
                    start, end = bounds(pool, e)
                    with pool.Fori(start, end) as b:
                        chain.enter(first + PER * b)
                        pool.wait_ge(resid_ready, b + 2)
                        pool.wait_ge(xn_ready, b + 2)
                        chain.apart()
                        gather(b + 2)
                        write(b)
                        coefs(b + 2)
                        assert chain.n == PER, chain.n
            blocks = bounds(pool, NEXP - 1)[1]
            chain.enter(first + PER * blocks)
            write(blocks)
            pool.wait_ge(written, 80 * blocks + 96)
            pool.wait_ge(gathered, 80 * blocks + 160)

        @block.scalar
        def _(act):
            def split_high(e, s):
                for n in range(2):
                    act.wait_ge(raw_in[n], 16 * e + 16)
                nc.scalar.copy(w_hi[s][:], raw[:]).then_inc(hi_ready, 1)

            def take_high(b, i):
                act.wait_ge(turned, BT * b + (i + 2))
                nc.scalar.copy(x_hi[:, :, i * P:(i + 1) * P],
                               ps_x[:, i % 2, :D].rearrange("p (k t) -> p k t", k=2)).then_inc(x_hi_ready, 1)

            act.sem_inc(h_hi_ready, 2)
            act.wait_ge(cleared, 1)
            act.sem_inc(y_all_ready, 1)
            split_high(0, 0)
            for i in range(BT):
                take_high(0, i)
            with act.Fori(0, NEXP // 2) as pair:
                for s in range(2):
                    e = 2 * pair + s
                    start, end = bounds(act, e)
                    act.wait_ge(y_all_ready, BT * start + 1)
                    split_high(e + 1, 1 - s)
                    with act.Fori(start, end) as b:
                        for f in range(KF):
                            h = f % 2
                            act.wait_ge(h_ready, KF * b + (f + 1))
                            act.wait_ge(h_lo_ready, KF * b + (f + 1))
                            nc.scalar.activation(h_all[h][:].rearrange("p (m t) -> p m t", m=2), ps_h[:, h, :, :HB],
                                                 ACT.Relu, bias=b1[:, e, f:f + 1])
                            nc.scalar.activation(h_hi[:, f].rearrange("p (m t) -> p m t", m=2), ps_h[:, h, :, :HB],
                                                 ACT.Relu, bias=b1[:, e, f:f + 1]).then_inc(h_hi_ready, 1)
                            if f == 0:
                                act.wait_ge(below_ready, b + 1)
                                nc.scalar.activation(power_e[:], below[:], ACT.Exp).then_inc(exp_ready, 1)
                        take_high(b + 1, 0)
                        take_high(b + 1, 1)
                        act.wait_ge(prob_ready, b + 1)
                        act.wait_ge(clean_ready, b + 1)
                        for i in range(BT):
                            act.wait_ge(y_sum_ready, BT * b + (i + 2))
                            nc.scalar.activation(y_all[:, i], y_sum[:, i % 2], ACT.Copy,
                                                 scale=prob[:, i:i + 1]).then_inc(y_all_ready, 1)
                            if 1 <= i < BT - 1:
                                take_high(b + 1, i + 1)

        @block.tensor
        def _(pe):
            def turn(b, i):
                if i == 0:
                    pe.wait_ge(xn_ready, b + 1)
                pe.wait_ge(logits_taken, BT * b + (i + (i == 0)))
                for c in range(2):
                    ins = nc.tensor.transpose(ps_x[:, i % 2, c * P:(c + 1) * P], xn[:, i, c * P:(c + 1) * P],
                                              ident[:])
                ins.then_inc(turned, 1)

            def gate(b, i):
                pe.wait_ge(x_hi_ready, BT * b + (i + 1))
                pe.wait_ge(x_lo_ready, BT * b + (i + 1))
                tile = slice(i * P, (i + 1) * P)
                for c in range(2):
                    nc.tensor.matmul(ps_x[:, i % 2, D:D + 2 * NEXP], x_hi[:, c, tile],
                                     gate_parts[:, c].rearrange("p h e -> p (h e)"), start=c == 0, stop=False)
                for c in range(2):
                    ins = nc.tensor.matmul(ps_x[:, i % 2, D:D + NEXP], x_lo[:, c, tile],
                                           gate_parts[:, c, 0], start=False, stop=c == 1)
                ins.then_inc(logits_ready, 1)

            def up(b, s, f):
                h = f % 2
                pe.wait_ge(h_hi_ready, KF * b + (f + 1))
                n = 0
                for c in range(2):
                    w = slice(c * HID + f * P, c * HID + (f + 1) * P)
                    for weights, x in ((w_hi, x_hi), (w_hi, x_lo), (w_lo, x_hi)):
                        for m in range(2):
                            ins = nc.tensor.matmul(ps_h[:, h, m, :HB], weights[s][:, w],
                                                   x[:, c, m * HB:(m + 1) * HB], start=n == 0, stop=n == 5)
                        n += 1
                ins.then_inc(h_ready, 1)

            def down(b, s, i):
                pe.wait_ge(y_sum_ready, BT * b + (i + (i == 0)))
                n = 0
                for f in range(KF):
                    if i == 0:
                        pe.wait_ge(h_hi_ready, KF * b + (f + 3))
                        pe.wait_ge(h_lo_ready, KF * b + (f + 3))
                    w = slice(W1 + f * D, W1 + (f + 1) * D)
                    for x, weights in ((h_hi, w_hi), (h_hi, w_lo), (h_lo, w_hi)):
                        ins = nc.tensor.matmul(ps_y[:, i % 2, :D], x[:, f, i * P:(i + 1) * P], weights[s][:, w],
                                               start=n == 0, stop=n == 3 * KF - 1)
                        n += 1
                ins.then_inc(y_ready, 1)

            pe.sem_inc(turned, 1)
            pe.wait_ge(consts_in, CONSTS)
            pe.wait_ge(gate_ready, 1)
            for i in range(BT):
                turn(0, i)
                gate(0, i)
            with pe.Fori(0, NEXP // 2) as pair:
                for s in range(2):
                    e = 2 * pair + s
                    start, end = bounds(pe, e)
                    with pe.Fori(start, end) as b:
                        pe.wait_ge(hi_ready, e + 1)
                        pe.wait_ge(lo_ready, e + 1)
                        for f in range(KF):
                            up(b, s, f)
                        turn(b + 1, 0)
                        turn(b + 1, 1)
                        for i in range(BT):
                            down(b, s, i)
                            gate(b + 1, i)
                            if 1 <= i < BT - 1:
                                turn(b + 1, i + 1)

        @block.vector
        def _(v):
            chain = Chain(v, step_dve, spare_dve)
            tt, ts, stt, red = (nc.vector.tensor_tensor, nc.vector.tensor_scalar,
                                nc.vector.scalar_tensor_tensor, nc.vector.tensor_reduce)

            def statistics(b):
                v.wait_ge(gathered, 80 * b + 80)
                for i in range(BT):
                    ins = nc.vector.bn_stats(stats[:, i], xg[:, i])
                chain.link(ins)
                for i in range(BT):
                    ins = nc.vector.bn_aggr(mv[:, i], stats[:, i])
                ins.then_inc(mv_ready, 1)

            def normalise(b, tiles):
                if 0 in tiles:
                    v.wait_ge(coef_ready, b + 1)
                    v.wait_ge(turned, BT * b + 1)
                for i in tiles:
                    ins = ts(xn[:, i], xg[:, i], rstd[:, i:i + 1], shift[:, i:i + 1], ALU.mult, ALU.add)
                if BT - 1 in tiles:
                    ins.then_inc(xn_ready, 1)

            def keep(b):
                v.wait_ge(done_ready, b)
                nc.vector.tensor_copy(resid[:, bass.ds(b % 3, 1)], xg[:].unsqueeze(1)).then_inc(resid_ready, 1)

            def take_low(b, i):
                v.wait_ge(x_hi_ready, BT * b + (i + 1))
                tt(x_lo[:, :, i * P:(i + 1) * P], ps_x[:, i % 2, :D].rearrange("p (k t) -> p k t", k=2),
                   x_hi[:, :, i * P:(i + 1) * P].bitcast(F32), ALU.subtract).then_inc(x_lo_ready, 1)

            def take_logits(b, i):
                v.wait_ge(logits_ready, BT * b + (i + 1))
                nc.vector.tensor_copy(logit_parts[:, i], ps_x[:, i % 2, D:D + 2 * NEXP]).then_inc(logits_taken, 1)

            v.wait_ge(consts_in, CONSTS)
            gate_2 = gate_raw[:].rearrange("p (k e) -> p k e", k=2)
            chain.link(nc.vector.tensor_copy(gate_parts[:, :, 0], gate_2))
            tt(gate_parts[:, :, 1], gate_2, gate_parts[:, :, 0].bitcast(F32), ALU.subtract).then_inc(gate_ready, 1)
            v.sem_inc(y_sum_ready, 1)
            v.sem_inc(logits_taken, 1)
            v.sem_inc(h_lo_ready, 2)
            statistics(0)
            v.wait_ge(coef_ready, 1)
            for i in range(BT):
                ins = ts(xn[:, i], xg[:, i], rstd[:, i:i + 1], shift[:, i:i + 1], ALU.mult, ALU.add)
            ins.then_inc(xn_ready, 1)
            nc.vector.tensor_copy(resid[:, 0], xg[:]).then_inc(resid_ready, 1)
            for i in range(BT):
                take_low(0, i)
                take_logits(0, i)
            statistics(1)

            first = chain.n
            PER = 3 + 1 + 4 + 1

            def infinite_above(b):
                v.wait_ge(y_all_ready, BT * b + 1)
                v.wait_ge(done_ready, b + 1)
                chain.mark(ts(clean[:], y_all[:], LARGEST, 1e4, ALU.is_gt, ALU.mult))

            def infinite_below():
                chain.mark(ts(negative[:], y_all[:], -LARGEST, -1e4, ALU.is_lt, ALU.mult))

            def find_finite():
                chain.mark(ts(finite[:], y_all[:], 0.0, 0.0, ALU.mult, ALU.is_equal))

            def keep_finite():
                chain.wait()
                chain.link(tt(clean[:], clean[:], negative[:], ALU.add))
                nc.vector.copy_predicated(clean[:], finite[:], y_all[:]).then_inc(clean_ready, 1)

            with v.Fori(0, NEXP // 2) as pair:
                for s in range(2):
                    e = 2 * pair + s
                    start, end = bounds(v, e)
                    with v.Fori(start, end) as b:
                        chain.enter(first + PER * b)
                        v.wait_ge(logits_taken, BT * b + (BT + 1))
                        chain.link(tt(logits_sum[:], logit_parts[:, :, :NEXP], logit_parts[:, :, NEXP:], ALU.add))
                        chain.link(tt(logits[:], logits_sum[:], gate_b[:].unsqueeze(1).broadcast_to([P, BT, NEXP]),
                                      ALU.add))
                        chain.link(red(top[:], logits[:], AX.X, ALU.max))
                        tt(below[:], logits[:], top[:].unsqueeze(2).broadcast_to([P, BT, NEXP]),
                           ALU.subtract).then_inc(below_ready, 1)
                        for f in range(KF):
                            v.wait_ge(h_hi_ready, KF * b + (f + 3))
                            tt(h_lo[:, f], h_all[f % 2][:], h_hi[:, f].bitcast(F32),
                               ALU.subtract).then_inc(h_lo_ready, 1)
                            if f < 3:
                                normalise(b + 1, range(2 * f, min(2 * f + 2, BT)))
                            if f == 1:
                                v.wait_ge(exp_ready, b + 1)
                                v.wait_ge(y_all_ready, BT * b + 1)
                                chain.link(red(total[:], power_e[:], AX.X, ALU.add))
                                nc.vector.reciprocal(prob[:], total[:]).then_inc(prob_ready, 1)
                            if f == 3:
                                keep(b + 1)
                            if f == 4:
                                infinite_above(b)
                            if f == 5:
                                infinite_below()
                            if f == 6:
                                find_finite()
                        take_low(b + 1, 0)
                        take_low(b + 1, 1)
                        keep_finite()
                        for i in range(BT):
                            v.wait_ge(y_ready, BT * b + (i + 1))
                            v.wait_ge(y_all_ready, BT * b + (i + (i == 0)))
                            tt(y_sum[:, i % 2], ps_y[:, i % 2, :D], b2[:, e], ALU.add).then_inc(y_sum_ready, 1)
                            take_logits(b + 1, i)
                            if 1 <= i < BT - 1:
                                take_low(b + 1, i + 1)
                            if i == 1:
                                statistics(b + 2)
                        assert chain.n == PER, chain.n
            blocks = bounds(v, NEXP - 1)[1]
            chain.enter(first + PER * blocks)
            infinite_above(blocks)
            infinite_below()
            find_finite()
            keep_finite()




def build(nc, io, out):
    with ExitStack() as ctx:
        def table(name, shape):
            return ctx.enter_context(nc.sbuf_tensor(name, shape, I32))

        take_row = table("take_row", [P, NST + 2 * BT])
        put_row = table("put_row", [P, BT + NST])
        first_block = table("first_block", [1, NEXP + 1])
        edge_and_node_block(nc, io, out)
        routing_block(nc, io, out, take_row, put_row, first_block)
        expert_block(nc, io, out, take_row, put_row, first_block)


def layout(x, src, dst, ea3, ea8, w):
    f = np.float32
    pad = EPAD - NE
    own = np.arange(GR)
    xp = np.concatenate([x, np.zeros((ROWS - NN, D), f)])
    srcp = np.concatenate([src, np.zeros(pad, np.int32)]).astype(np.int32)
    dstp = np.concatenate([dst, (ROWS + np.arange(NE, EPAD) % GR)]).astype(np.int32)
    ea3p = np.concatenate([ea3, np.zeros((pad, 3), f)])
    ea8p = np.concatenate([ea8, np.zeros((pad, 8), f)])
    lin = np.zeros((D, D), f)
    lin[:MUL, :MUL] = w["L0_gnn_lin_w0"]
    for i in range(3):
        lin[MUL + i::3, MUL + i::3] = w["L0_gnn_lin_w1"]
    t = np.arange(NT)
    p = np.arange(P)[:, None]
    return {
        "gate_w": w["L0_ffn_gate_w"].reshape(2, P, NEXP).transpose(1, 0, 2),
        "gate_b": np.broadcast_to(w["L0_ffn_gate_b"], (P, NEXP)),
        "w1": w["L0_ffn_w1"],
        "w2": w["L0_ffn_w2"],
        "b1": w["L0_ffn_b1"].reshape(NEXP, HID // P, P).transpose(2, 0, 1),
        "b2": w["L0_ffn_b2"].reshape(1, NEXP * D),
        "ident": np.eye(P, dtype=f),
        "valid": (t * P + p < NN).astype(f),
        "tile_no": np.broadcast_to(t, (P, NT)).astype(f),
        "row_no": (p + 1).astype(f),
        "falling": np.broadcast_to(NEXP - np.arange(NEXP), (P, NEXP)).astype(f),
        "thresholds": np.broadcast_to(BR * np.arange(EB), (P, EB)).astype(f),
        "before": (np.arange(P) > p).astype(f),
        "iota": np.broadcast_to(np.arange(256), (P, 256)).astype(f),
        "ones_row": np.ones((P, NT), f),
        "x": xp,
        "dst": dstp,
        "src_tiles": srcp.reshape(-1, P).T,
        "dst_tiles": dstp[:EG * GR].reshape(-1, P).T,
        "vec_tiles": ea3p.reshape(-1, P, 3).transpose(1, 0, 2),
        "emb": ea8p.reshape(-1, GR, 8).transpose(0, 2, 1),
        "trash": (ROWS + own).reshape(GT, P).T.astype(f),
        "upper": (own[None] >= np.arange(P)[:, None]).astype(f),
        "lin": lin.reshape(2, P, D).transpose(1, 0, 2),
        "fc1": w["L0_gnn_fc_w1"],
        "fc2": w["L0_gnn_fc_w2"],
    }


def kernel(x, src, dst, edge_attr_3, edge_attr_8, **w):
    import concourse.bacc as bacc
    from concourse.bass_utils import run_bass_kernel_spmd

    nc = bacc.Bacc("TRN2", target_bir_lowering=False, num_devices=1)
    w = {k: np.asarray(a) for k, a in w.items()}
    arrays = layout(*(np.asarray(a) for a in (x, src, dst, edge_attr_3, edge_attr_8)), w)
    arrays = {k: np.ascontiguousarray(a) for k, a in arrays.items()}
    io = {k: nc.dram_tensor(f"in_{k}", a.shape, mybir.dt.from_np(a.dtype), kind="ExternalInput").ap()
          for k, a in arrays.items()}
    out = nc.dram_tensor("out", (ROWS + GR, D), F32, kind="ExternalOutput").ap()
    io["spare"] = nc.dram_tensor("spare", (P, D), F32).ap()
    build(nc, io, out)
    r = run_bass_kernel_spmd(nc, [{f"in_{k}": a for k, a in arrays.items()}], core_ids=[0])
    return r.results[0]["out"][:NN]
```

```python
from contextlib import ExitStack

import numpy as np

import concourse.bass as bass
from concourse import mybir

ALU = mybir.AluOpType
ACT = mybir.ActivationFunctionType
AX = mybir.AxisListType
F32 = mybir.dt.float32
F32R = mybir.dt.float32r
BF16 = mybir.dt.bfloat16
I32 = mybir.dt.int32
U32 = mybir.dt.uint32

P = 128
D = 256
MUL = 64
NN, NE = 20000, 10000
GT = 4
GR = GT * P
NG = -(-NN // GR)
NT = NG * GT
ROWS = NG * GR
EG = -(-NE // GR)
EPAD = (EG + 4) * GR
NEXP, HID = 8, 1024
CAP = -(-5 * NN // (4 * NEXP))
BT = 5
BR = BT * P
EB = -(-CAP // BR)
NB = NEXP * EB
EST = EB * BT
NST = NEXP * EST
EPS = 1e-5
LARGEST = float(np.finfo(np.float32).max)
TABLES = 16 * 8
AHALF = NG // 4
UG = AHALF + 1


class Chain:

    def __init__(self, engine, sem, spare=None):
        self.engine, self.sem, self.base, self.n, self.spare = engine, sem, 0, 0, spare

    def apart(self):
        self.engine.sem_inc(self.spare, 1)

    def mark(self, ins):
        ins.then_inc(self.sem, 1)
        self.n += 1
        return ins

    def wait(self, back=0):
        self.engine.wait_ge(self.sem, self.base + (self.n - back))

    def link(self, ins):
        self.mark(ins)
        self.wait()
        if self.spare is not None:
            self.apart()

    def enter(self, base):
        self.base, self.n = base, 0


class Constants:

    def __init__(self, ctx, nc, io):
        self.io = io
        self.tiles = {}
        for name, shape in (
            ("ident", [P, P]),
            ("gate_w", [P, 2, NEXP]),
            ("gate_b", [P, NEXP]),
            ("valid", [P, NT]),
            ("tile_no", [P, NT]),
            ("row_no", [P, 1]),
            ("falling", [P, NEXP]),
            ("thresholds", [P, EB]),
            ("before", [P, P]),
            ("iota", [P, 256]),
            ("ones_row", [P, NT]),
            ("b1", [P, NEXP, HID // P]),
        ):
            self.tiles[name] = ctx.enter_context(nc.sbuf_tensor(f"c_{name}", shape, F32))
        self.loaded = ctx.enter_context(nc.semaphore("constants_loaded"))

    def load(self, sp):
        for name, tile in self.tiles.items():
            sp.dma_start(tile[:], self.io[name]).then_inc(self.loaded, 16)

    def wait(self, engine):
        engine.wait_ge(self.loaded, 16 * len(self.tiles))

    def __getitem__(self, name):
        return self.tiles[name]


def edge_and_node_block(nc, io, x1, constants):
    assert NG % 4 == 0 and EG == 2 * AHALF and EG % 2 == 0
    with ExitStack() as ctx:
        def sb(name, shape, dt=F32):
            return ctx.enter_context(nc.sbuf_tensor(name, shape, dt))

        def ps(name, shape, dt=F32):
            return ctx.enter_context(nc.psum_tensor(name, shape, dt))

        def sem(name):
            return ctx.enter_context(nc.semaphore(name))

        src = sb("src", [P, EPAD // P], I32)
        dst_col = sb("dst_col", [P, EG * GT], I32)
        dst_f = sb("dst_f", [P, EG * GT])
        dst_less_trash = sb("dst_less_trash", [P, EG * GT])
        trash = sb("trash", [P, GT])
        edge_vec = sb("edge_vec", [P, EPAD // P, 3])
        edge_sq = sb("edge_sq", [P, EPAD // P, 3])
        len_now = [sb(f"len_now{h}", [P, GT]) for h in range(2)]
        len_eps = sb("len_eps", [P, GT])
        inv_len = sb("inv_len", [P, GT])
        edge_len = sb("edge_len", [P, EPAD // P])
        half = sb("half", [P, EPAD // P])
        minus_half = sb("minus_half", [P, 16])
        edge_dir = sb("edge_dir", [P, EPAD // P, 4])
        upper = sb("upper", [P, GR])
        lin = sb("lin", [P, 2, D])
        fc1 = sb("fc1", [8, MUL])
        fc2 = sb("fc2", [MUL, 5 * MUL])
        src_now = [sb(f"src_now{h}", [P, GT], I32) for h in range(2)]
        row_now = [sb(f"row_now{h}", [P, GT], I32) for h in range(2)]
        upd_now = [[sb(f"upd_now{h}{s}", [P, GT, D]) for s in range(2)] for h in range(2)]
        xin = [sb(f"xin{h}", [P, 4, GT, D]) for h in range(2)]
        node_stats = sb("node_stats", [P, 4 * GT, 6])
        node_mv = sb("node_mv", [P, 4 * GT, 2])
        node_var = sb("node_var", [P, 4 * GT])
        node_rstd = sb("node_rstd", [P, 4 * GT])
        node_minus_rstd = sb("node_minus_rstd", [P, 4 * GT])
        node_scale = [sb(f"node_scale{h}", [P, 4 * GT]) for h in range(2)]
        node_bias = [sb(f"node_bias{h}", [P, 4 * GT]) for h in range(2)]
        xe = [sb(f"xe{h}", [P, GT, D]) for h in range(2)]
        edge_stats = sb("edge_stats", [P, GT, 6])
        edge_mv = sb("edge_mv", [P, GT, 2])
        edge_var = sb("edge_var", [P, GT])
        edge_rstd = sb("edge_rstd", [P, GT])
        edge_minus_rstd = sb("edge_minus_rstd", [P, GT])
        edge_shift = sb("edge_shift", [P, GT])
        coef_scale = [sb(f"coef_scale{h}", [P, GT, 4]) for h in range(2)]
        coef_bias = [sb(f"coef_bias{h}", [P, GT, 4]) for h in range(2)]
        y = [sb(f"y{h}", [P, GT, 4, D]) for h in range(2)]
        dst_row = [sb(f"dst_row{h}", [P, GR], I32) for h in range(2)]
        emb = [sb(f"emb{h}", [8, GR]) for h in range(2)]
        hidden = sb("hidden", [MUL, GR])
        same = [sb(f"same{h}", [P, GT, GR]) for h in range(2)]
        later = sb("later", [P, GT])
        pick = sb("pick", [P, GT])
        msg = [sb(f"msg{h}", [P, GT, D]) for h in range(2)]
        tmp_a = sb("tmp_a", [P, GT, 3 * MUL])
        tmp_b = sb("tmp_b", [P, GT, 3 * MUL])
        tmp_c = sb("tmp_c", [P, GT, 3 * MUL])
        tmp_d = sb("tmp_d", [P, GT, MUL])
        tmp_e = sb("tmp_e", [P, GT, MUL])
        tmp_f = sb("tmp_f", [P, GT, MUL])
        done = sb("done", [P, 1])
        tmp_g = sb("tmp_g", [P, GT, 3 * MUL])
        tmp_h = sb("tmp_h", [P, GT, 3 * MUL])
        agg = sb("agg", [P, 2, GR])
        upd = sb("upd", [P, UG * GT, D])
        upd_row = sb("upd_row", [P, EG * GT], I32)

        ps_w = ps("ps_w", [P, GT, 512])
        ps_h = ps("ps_h", [MUL, GR])
        ps_agg = ps("ps_agg", [P, 2, GR])
        ps_lin = ps("ps_lin", [P, 2, D])

        tables_in = sem("tables_in")
        x_in = [[sem(f"x_in{h}{a}") for a in range(4)] for h in range(2)]
        x1_out = [[sem(f"x1_out{h}{a}") for a in range(4)] for h in range(2)]
        dst_in = [sem(f"dst_in{h}") for h in range(2)]
        emb_in = [sem(f"emb_in{h}") for h in range(2)]
        gathered = [sem(f"gathered{h}") for h in range(2)]
        scattered = sem("scattered")
        dve_step = sem("dve_step")
        pool_step = sem("pool_step")
        pool_spare = sem("pool_spare")
        dve_spare = sem("dve_spare")
        node_mv_ready = sem("node_mv_ready")
        node_coef_ready = sem("node_coef_ready")
        act_rows_ready = sem("act_rows_ready")
        pool_rows_ready = sem("pool_rows_ready")
        len_ready = sem("len_ready")
        dir_ready = sem("dir_ready")
        weights_ready = sem("weights_ready")
        edge_mv_ready = sem("edge_mv_ready")
        coef_ready = sem("coef_ready")
        now_ready = sem("now_ready")
        pairs_added = sem("pairs_added")
        y_ready = sem("y_ready")
        same_ready = sem("same_ready")
        msg_ready = sem("msg_ready")
        row_ready = sem("row_ready")
        ps_h_ready = sem("ps_h_ready")
        hidden_ready = sem("hidden_ready")
        ps_w_ready = sem("ps_w_ready")
        ps_agg_ready = sem("ps_agg_ready")
        agg_ready = sem("agg_ready")
        ps_lin_ready = sem("ps_lin_ready")
        upd_ready = sem("upd_ready")

        x_v = io["x"].rearrange("(g t p) c -> g p t c", t=GT, p=P)
        x1_v = x1.rearrange("(g t p) c -> g p t c", t=GT, p=P)
        dst_v = io["dst"].rearrange("(g c) -> g c", c=GR)

        block = ctx.enter_context(nc.Block())

        @block.sync
        def _(sp):
            def load_rows(q, h):
                for a in range(4):
                    sp.dma_start(xin[h][:, a], x_v[4 * q + a]).then_inc(x_in[h][a], 16)

            def store_rows(q, h):
                for a in range(4):
                    if a < 2:
                        sp.wait_ge(act_rows_ready, 2 * q + (a + 1))
                    else:
                        sp.wait_ge(pool_rows_ready, 2 * q + (a - 1))
                    sp.dma_start(x1_v[4 * q + a], xin[h][:, a]).then_inc(x1_out[h][a], 16)

            def load_embedding(q, h):
                sp.dma_start(emb[h][:], io["emb"][q]).then_inc(emb_in[h], 16)

            def load_receivers(q, h):
                sp.dma_start(dst_row[h][:], dst_v[bass.ds(q, 1)].broadcast_to([P, GR])).then_inc(dst_in[h], 16)

            sp.dma_start(src[:], io["src_tiles"]).then_inc(tables_in, 16)
            sp.dma_start(dst_col[:], io["dst_tiles"]).then_inc(tables_in, 16)
            sp.dma_start(edge_vec[:], io["vec_tiles"]).then_inc(tables_in, 16)
            load_rows(0, 0)
            for h in range(2):
                load_embedding(h, h)
                load_receivers(h, h)
            load_rows(1, 1)
            constants.load(sp)

            def next_edges(q, h):
                sp.wait_ge(same_ready, q + 1)
                load_receivers(q + 2, h)

            def step(k, h, nodes, more):
                q = 2 * k + h
                sp.wait_ge(ps_h_ready, q + 1)
                load_embedding(q + 2, h)
                if nodes:
                    store_rows(q, h)
                if more:
                    for a in range(4):
                        sp.wait_ge(x1_out[h][a], 16 * k + 16)
                    load_rows(q + 2, h)
                next_edges(q, h)

            with sp.Fori(0, AHALF // 2 - 1) as k:
                for h in range(2):
                    step(k, h, True, True)
            for h in range(2):
                step(AHALF // 2 - 1, h, True, False)
            with sp.Fori(AHALF // 2, EG // 2) as k:
                for h in range(2):
                    step(k, h, False, False)
            constants.wait(sp)
            for h in range(2):
                sp.wait_ge(emb_in[h], 16 * (EG // 2 + 1))
                sp.wait_ge(dst_in[h], 16 * (EG // 2 + 1))
            sp.wait_ge(scattered, 64 * (EG + 1))
            for h in range(2):
                for a in range(4):
                    sp.wait_ge(x1_out[h][a], 16 * AHALF // 2)

        @block.gpsimd
        def _(pool):
            chain = Chain(pool, pool_step, pool_spare)

            def gather(q, h):
                chain.link(nc.gpsimd.tensor_copy(src_now[h][:], src[:, bass.ds(GT * q, GT)]))
                for t in range(GT):
                    nc.gpsimd.indirect_dma_start(
                        xe[h][:, t, :], None, io["x"],
                        bass.IndirectOffsetOnAxis(src_now[h][:, t:t + 1].bitcast(U32), 0),
                        bounds_check=NN - 1,
                    ).then_inc(gathered[h], 16)

            def affine_coefs(mv, var, rstd, minus_rstd, n):
                chain.link(nc.gpsimd.tensor_scalar(var[:], mv[:, :, 1], EPS, None, ALU.add))
                chain.link(nc.gpsimd.tensor_tensor(rstd[:], var[:], minus_half[:, :n], ALU.pow))
                chain.link(nc.gpsimd.tensor_scalar(minus_rstd[:], rstd[:], -1.0, None, ALU.mult))

            def edge_coefs(q, h):
                pool.wait_ge(edge_mv_ready, q + 1)
                chain.apart()
                affine_coefs(edge_mv, edge_var, edge_rstd, edge_minus_rstd, GT)
                chain.link(nc.gpsimd.tensor_tensor(edge_shift[:], edge_mv[:, :, 0], edge_minus_rstd[:], ALU.mult))
                direction = edge_dir[:, bass.ds(GT * q, GT), :]
                nc.gpsimd.tensor_tensor(coef_scale[h][:], direction,
                                        edge_rstd[:].unsqueeze(2).broadcast_to([P, GT, 4]), ALU.mult)
                nc.gpsimd.tensor_tensor(coef_bias[h][:], direction,
                                        edge_shift[:].unsqueeze(2).broadcast_to([P, GT, 4]),
                                        ALU.mult).then_inc(coef_ready, 1)

            def node_rows(q, h):
                pool.wait_ge(node_mv_ready, q + 1)
                chain.apart()
                affine_coefs(node_mv, node_var, node_rstd, node_minus_rstd, 4 * GT)
                chain.link(nc.gpsimd.tensor_scalar(node_scale[h][:], node_rstd[:], 1.0, None, ALU.add))
                nc.gpsimd.tensor_tensor(node_bias[h][:], node_mv[:, :, 0], node_minus_rstd[:],
                                        ALU.mult).then_inc(node_coef_ready, 1)
                pool.wait_ge(node_coef_ready, q + 2)
                chain.apart()
                for a in (2, 3):
                    for t in range(GT):
                        c = a * GT + t
                        ins = nc.gpsimd.tensor_scalar(xin[h][:, a, t], xin[h][:, a, t], node_scale[h][:, c:c + 1],
                                                      node_bias[h][:, c:c + 1], ALU.mult, ALU.add)
                    ins.then_inc(pool_rows_ready, 1)

            def scatter(g, h, s):
                pool.wait_ge(now_ready, g + 1)
                pool.wait_ge(row_ready, g + 1)
                chain.apart()
                chain.link(nc.gpsimd.tensor_copy(row_now[s][:], upd_row[:, bass.ds(GT * g, GT)]))
                pool.wait_ge(scattered, 64 * g + 64)
                if s == 0:
                    pool.sem_inc(pairs_added, 1)
                else:
                    chain.apart()
                for t in range(GT):
                    nc.gpsimd.indirect_dma_start(
                        x1, bass.IndirectOffsetOnAxis(row_now[s][:, t:t + 1].bitcast(U32), 0),
                        upd_now[h][s][:, t, :], None, bounds_check=ROWS + GR - 1, compute_op=ALU.add,
                    ).then_inc(scattered, 16)

            def read_ahead(q, h):
                pool.wait_ge(y_ready, q - 1)
                chain.apart()
                gather(q, h)

            pool.sem_inc(pairs_added, 1)
            nc.gpsimd.memset(half[:], 0.5)
            nc.gpsimd.memset(minus_half[:], -0.5)
            chain.mark(nc.gpsimd.memset(y[1][:], 0.0))
            pool.wait_ge(pool_step, 1)
            for t in range(GT):
                pool.dma_start(x1_v[NG, :, t], y[1][:, t, 0, :]).then_inc(scattered, 16)
            pool.wait_ge(dve_step, 2)
            near = slice(0, 3 * GT)
            nc.gpsimd.tensor_tensor(edge_len[:, near], edge_len[:, near], half[:, near],
                                    ALU.pow).then_inc(len_ready, 1)
            gather(0, 0)
            gather(1, 1)
            pool.wait_ge(dir_ready, 1)
            edge_coefs(0, 0)
            edge_coefs(1, 1)
            read_ahead(2, 0)

            def length(q, h):
                if not isinstance(q, int) or q >= 0:
                    pool.wait_ge(dir_ready, q + 1)
                    chain.apart()
                nc.gpsimd.tensor_tensor(len_now[h][:], edge_len[:, bass.ds(GT * (q + 4), GT)], half[:, :GT],
                                        ALU.pow).then_inc(len_ready, 1)

            def prepare(q, h):
                pool.wait_ge(dir_ready, q + 1)
                edge_coefs(q + 2, h)
                read_ahead(q + 3, 1 - h)

            def step(q, h):
                g = 2 * (q - AHALF)
                length(q, h)
                prepare(q, h)
                scatter(g, h, 0)
                scatter(g + 1, h, 1)

            length(-1, 1)
            first = chain.n
            per = 4 + 4 + 1
            with pool.Fori(0, AHALF // 2) as k:
                for h in range(2):
                    chain.enter(first + (2 * k + h) * per)
                    length(2 * k + h, h)
                    node_rows(2 * k + h, h)
                    prepare(2 * k + h, h)
                    assert chain.n == per, chain.n
            first += AHALF * per
            for h in range(2):
                for a in range(4):
                    pool.wait_ge(x1_out[h][a], 16 * AHALF // 2)
            per = 4 + 1 + 2
            with pool.Fori(AHALF // 2, EG // 2 - 1) as k:
                for h in range(2):
                    chain.enter(first + (2 * k + h - AHALF) * per)
                    step(2 * k + h, h)
                    assert chain.n == per, chain.n
            chain.enter(first + (EG - 2 - AHALF) * per)
            step(EG - 2, 0)
            length(EG - 1, 1)
            for s in range(2):
                scatter(EG - 2 + s, 1, s)
            pool.wait_ge(scattered, 64 * (EG + 1))
            for h in range(2):
                pool.wait_ge(gathered[h], 64 * (EG // 2 + 1))

        @block.scalar
        def _(act):
            def rows_times_direction(h, tiles):
                for t in tiles:
                    for j in range(4):
                        ins = nc.scalar.activation(y[h][:, t, j, :], xe[h][:, t, :], ACT.Identity,
                                                   bias=coef_bias[h][:, t, j:j + 1],
                                                   scale=coef_scale[h][:, t, j:j + 1])
                if GT - 1 in tiles:
                    ins.then_inc(y_ready, 1)

            def radial_hidden(q):
                act.wait_ge(ps_h_ready, q + 1)
                nc.scalar.activation(hidden[:], ps_h[:], ACT.Silu, scale=8 ** -0.5).then_inc(hidden_ready, 1)

            for tile, name in ((trash, "trash"), (fc1, "fc1"), (fc2, "fc2"), (lin, "lin"), (upper, "upper")):
                act.dma_start(tile[:], io[name]).then_inc(tables_in, 16)
            radial_hidden(0)
            act.wait_ge(coef_ready, 1)
            rows_times_direction(0, range(GT))
            act.wait_ge(ps_w_ready, 1)
            radial_hidden(1)
            act.wait_ge(scattered, 64)
            act.wait_ge(coef_ready, 2)
            rows_times_direction(1, range(GT))

            def rows_to_scatter(j, h, parts=(0, 1)):
                act.wait_ge(pairs_added, j + 1)
                act.wait_ge(upd_ready, 4 * j + (3 + 2 * parts[-1]))
                for s in parts:
                    nc.scalar.copy(upd_now[h][s][:],
                                   upd[:, bass.ds(GT * ((2 * j + s) % UG), GT), :]).then_inc(now_ready, 1)

            def step(k, h, nodes, pair=None, ahead=True, parts=(0, 1)):
                q = 2 * k + h
                if nodes:
                    act.wait_ge(node_coef_ready, q + 2)
                    for a in range(2):
                        for t in range(GT):
                            c = a * GT + t
                            ins = nc.scalar.activation(xin[h][:, a, t], xin[h][:, a, t], ACT.Identity,
                                                       bias=node_bias[h][:, c:c + 1],
                                                       scale=node_scale[h][:, c:c + 1])
                        ins.then_inc(act_rows_ready, 1)
                if pair is not None and ahead:
                    rows_to_scatter(pair, h)
                if ahead:
                    act.wait_ge(msg_ready, q + 2)
                    act.wait_ge(coef_ready, q + 3)
                    rows_times_direction(h, (0, 1))
                if pair is not None and not ahead:
                    rows_to_scatter(pair, h, parts)
                act.wait_ge(ps_w_ready, q + 2)
                radial_hidden(q + 2)
                act.wait_ge(ps_agg_ready, q + 3)
                nc.scalar.copy(agg[:, 0], ps_agg[:, 0])
                nc.scalar.copy(agg[:, 1], ps_agg[:, 1]).then_inc(agg_ready, 1)
                for s in range(2):
                    if ahead:
                        rows_times_direction(h, (2 + s,))
                    act.wait_ge(ps_lin_ready, 2 * q + (s + 1))
                    nc.scalar.copy(upd[:, bass.ds(GT * (q % UG) + 2 * s, 2), :], ps_lin[:]).then_inc(upd_ready, 1)

            with act.Fori(0, AHALF // 2) as k:
                for h in range(2):
                    step(k, h, True)
            with act.Fori(AHALF // 2, EG // 2 - 1) as k:
                for h in range(2):
                    step(k, h, False, 2 * k + h - AHALF)
            step(EG // 2 - 1, 0, False, AHALF - 2, ahead=False)
            step(EG // 2 - 1, 1, False, AHALF - 1, ahead=False, parts=(0,))
            rows_to_scatter(AHALF - 1, 1, (1,))

        @block.tensor
        def _(pe):
            def radial_first(q, k, h):
                pe.wait_ge(emb_in[h], 16 * k + 16)
                nc.tensor.matmul(ps_h[:], fc1[:], emb[h][:], start=True, stop=True).then_inc(ps_h_ready, 1)

            def radial_second():
                for t in range(GT):
                    ins = nc.tensor.matmul(ps_w[:, t, :5 * MUL], hidden[:, t * P:(t + 1) * P], fc2[:],
                                           start=True, stop=True)
                ins.then_inc(ps_w_ready, 1)

            pe.wait_ge(tables_in, TABLES)
            radial_first(0, 0, 0)
            pe.wait_ge(weights_ready, 1)
            pe.wait_ge(hidden_ready, 1)
            radial_second()
            radial_first(1, 0, 1)

            def step(k, h):
                q = 2 * k + h
                pe.wait_ge(hidden_ready, q + 2)
                pe.wait_ge(msg_ready, q + 2)
                radial_second()
                radial_first(q + 2, k + 1, h)
                pe.wait_ge(same_ready, q + 1)
                pe.wait_ge(agg_ready, q + 1)
                for c in range(2):
                    for t in range(GT):
                        ins = nc.tensor.matmul(ps_agg[:, c, t * P:], msg[h][:, t, c * P:(c + 1) * P],
                                               same[h][:, t, :GR - t * P], start=t == 0, stop=t == GT - 1)
                ins.then_inc(ps_agg_ready, 1)
                pe.wait_ge(agg_ready, q + 2)
                for s in range(2):
                    pe.wait_ge(upd_ready, 2 * q + (s + 1))
                    for t in (2 * s, 2 * s + 1):
                        for c in range(2):
                            ins = nc.tensor.matmul(ps_lin[:, t % 2], agg[:, c, t * P:(t + 1) * P], lin[:, c],
                                                   start=c == 0, stop=c == 1)
                    ins.then_inc(ps_lin_ready, 1)

            with pe.Fori(0, EG // 2) as k:
                for h in range(2):
                    step(k, h)

        @block.vector
        def _(v):
            chain = Chain(v, dve_step, dve_spare)

            def node_statistics(q, k, h):
                for a in range(4):
                    v.wait_ge(x_in[h][a], 16 * k + 16)
                    for t in range(GT):
                        ins = nc.vector.bn_stats(node_stats[:, a * GT + t], xin[h][:, a, t])
                chain.link(ins)
                v.wait_ge(node_coef_ready, q + 1)
                chain.apart()
                for c in range(4 * GT):
                    ins = nc.vector.bn_aggr(node_mv[:, c], node_stats[:, c])
                ins.then_inc(node_mv_ready, 1)

            def edge_statistics(q, k, h):
                v.wait_ge(gathered[h], 64 * k + 64)
                for t in range(GT):
                    ins = nc.vector.bn_stats(edge_stats[:, t], xe[h][:, t])
                chain.link(ins)
                for t in range(GT):
                    ins = nc.vector.bn_aggr(edge_mv[:, t], edge_stats[:, t])
                ins.then_inc(edge_mv_ready, 1)

            def receivers(q, k, h):
                v.wait_ge(dst_in[h], 16 * k + 16)
                v.wait_ge(ps_agg_ready, q + 1)
                for t in range(GT):
                    ins = nc.vector.scalar_tensor_tensor(
                        out=same[h][:, t, :GR - t * P], in0=dst_row[h][:, t * P:],
                        scalar=dst_f[:, bass.ds(GT * q + t, 1)], in1=upper[:, :GR - t * P],
                        op0=ALU.is_equal, op1=ALU.mult, accum_out=later[:, t:t + 1])
                ins.then_inc(same_ready, 1)
                v.wait_ge(same_ready, q + 1)
                chain.link(nc.vector.scalar_tensor_tensor(
                    out=pick[:], in0=later[:], scalar=1.0, in1=dst_less_trash[:, bass.ds(GT * q, GT)],
                    op0=ALU.is_equal, op1=ALU.mult))
                nc.vector.tensor_tensor(upd_row[:, bass.ds(GT * q, GT)], pick[:], trash[:],
                                        ALU.add).then_inc(row_ready, 1)

            def messages(q, h):
                v.wait_ge(y_ready, q + 1)
                v.wait_ge(ps_w_ready, q + 1)
                xs = y[h][:, :, :, :MUL]
                xv = y[h][:, :, :, MUL:].rearrange("p t j (u i) -> p t j u i", i=3)

                def vec(x):
                    return x[:].rearrange("p t (u i) -> p t u i", i=3)

                def w(n):
                    return ps_w[:, :, n * MUL:(n + 1) * MUL]

                def w3(n):
                    return w(n).unsqueeze(3).broadcast_to([P, GT, MUL, 3])

                tt = nc.vector.tensor_tensor
                chain.mark(tt(tmp_d[:], xv[:, :, 1, :, 0], xv[:, :, 2, :, 1], ALU.add))
                chain.mark(tt(tmp_e[:], xs[:, :, 0], w(0), ALU.mult))
                chain.mark(tt(vec(tmp_b), xv[:, :, 0], w3(2), ALU.mult))
                chain.mark(tt(vec(tmp_c), xs[:, :, 1:4].rearrange("p t j u -> p t u j"), w3(1), ALU.mult))
                chain.wait(3)
                chain.mark(tt(tmp_f[:], tmp_d[:], xv[:, :, 3, :, 2], ALU.add))
                for i in range(3):
                    a, b = (i + 1) % 3, (i + 2) % 3
                    chain.mark(tt(vec(tmp_a)[:, :, :, i], xv[:, :, b + 1, :, a], xv[:, :, a + 1, :, b],
                                  ALU.subtract))
                chain.wait(3)
                chain.mark(tt(tmp_d[:], tmp_f[:], w(3), ALU.mult))
                chain.mark(tt(tmp_g[:], tmp_b[:], tmp_c[:], ALU.add))
                chain.wait(2)
                chain.mark(tt(vec(tmp_h), vec(tmp_a), w3(4), ALU.mult))
                chain.wait(2)
                chain.mark(tt(msg[h][:, :, :MUL], tmp_e[:], tmp_d[:], ALU.add))
                chain.wait(1)
                chain.mark(tt(msg[h][:, :, MUL:], tmp_g[:], tmp_h[:], ALU.add))
                chain.wait()
                nc.vector.memset(done[:], 0.0).then_inc(msg_ready, 1)

            v.wait_ge(tables_in, TABLES)
            chain.link(nc.vector.tensor_tensor(edge_sq[:], edge_vec[:], edge_vec[:], ALU.mult))
            chain.link(nc.vector.tensor_reduce(edge_len[:], edge_sq[:], AX.X, ALU.add))
            nc.vector.tensor_copy(dst_f[:], dst_col[:]).then_inc(msg_ready, 1)
            nc.vector.tensor_scalar(lin[:], lin[:], 1 / (16 * 8), None, ALU.mult).then_inc(agg_ready, 1)
            for n, c in enumerate((2 ** -0.5, 3 ** -0.5, 3 ** -0.5, 6 ** -0.5, 6 ** -0.5)):
                ins = nc.vector.tensor_scalar(fc2[:, n * MUL:(n + 1) * MUL], fc2[:, n * MUL:(n + 1) * MUL],
                                              c / 8, None, ALU.mult)
            ins.then_inc(weights_ready, 1)
            v.wait_ge(msg_ready, 1)
            chain.link(nc.vector.tensor_tensor(
                dst_less_trash[:].rearrange("p (g t) -> p g t", t=GT),
                dst_f[:].rearrange("p (g t) -> p g t", t=GT),
                trash[:].unsqueeze(1).broadcast_to([P, EG, GT]), ALU.subtract))
            chain.link(nc.vector.tensor_scalar(edge_vec[:], edge_vec[:], 3 ** 0.5, None, ALU.mult))
            nc.vector.memset(edge_dir[:, :, 0:1], 1.0).then_inc(ps_agg_ready, 2)

            near = slice(0, 3 * GT)
            v.wait_ge(len_ready, 1)
            chain.link(nc.vector.tensor_scalar(edge_len[:, near], edge_len[:, near], 1e-9, None, ALU.add))
            chain.link(nc.vector.reciprocal(edge_len[:, near], edge_len[:, near]))
            nc.vector.tensor_tensor(edge_dir[:, near, 1:4], edge_vec[:, near],
                                    edge_len[:, near].unsqueeze(2).broadcast_to([P, 3 * GT, 3]),
                                    ALU.mult).then_inc(dir_ready, 1)
            nc.vector.memset(tmp_g[:], 0.0).then_inc(node_coef_ready, 1)
            nc.vector.memset(tmp_h[:], 0.0).then_inc(upd_ready, 1)
            edge_statistics(0, 0, 0)
            v.wait_ge(coef_ready, 1)
            edge_statistics(1, 0, 1)

            def directions(q, h):
                v.wait_ge(len_ready, q + 2)
                chain.apart()
                chain.link(nc.vector.tensor_scalar(len_eps[:], len_now[1 - h][:], 1e-9, None, ALU.add))
                chain.link(nc.vector.reciprocal(inv_len[:], len_eps[:]))
                cols = bass.ds(GT * (q + 3), GT)
                nc.vector.tensor_tensor(edge_dir[:, cols, 1:4], edge_vec[:, cols, :],
                                        inv_len[:].unsqueeze(2).broadcast_to([P, GT, 3]),
                                        ALU.mult).then_inc(dir_ready, 1)

            def step(k, h, nodes):
                q = 2 * k + h
                if nodes:
                    node_statistics(q, k, h)
                    receivers(q, k, h)
                    edge_statistics(q + 2, k + 1, h)
                    messages(q, h)
                else:
                    receivers(q, k, h)
                    messages(q, h)
                    edge_statistics(q + 2, k + 1, h)
                directions(q, h)

            first = chain.n
            per = 3 + 13 + 2
            with v.Fori(0, AHALF // 2) as k:
                for h in range(2):
                    chain.enter(first + (2 * k + h) * per)
                    step(k, h, True)
                    assert chain.n == per, chain.n
            first += AHALF * per
            per -= 1
            with v.Fori(AHALF // 2, EG // 2) as k:
                for h in range(2):
                    chain.enter(first + (2 * k + h - AHALF) * per)
                    step(k, h, False)
                    assert chain.n == per, chain.n


def routing_block(nc, io, x1, take_row, put_row, first_block, weights, constants):
    U = 4
    V = 8
    POOL = (2, 5, 7)
    DVE = [a for a in range(V) if a not in POOL]
    with ExitStack() as ctx:
        def sb(name, shape, dt=F32):
            return ctx.enter_context(nc.sbuf_tensor(name, shape, dt))

        def ps(name, shape, dt=F32):
            return ctx.enter_context(nc.psum_tensor(name, shape, dt))

        def sem(name):
            return ctx.enter_context(nc.semaphore(name))

        rows = sb("rows", [P, U, GT, D])
        stats = [sb(f"stats{h}", [P, GT, 6]) for h in range(2)]
        mv = [sb(f"mv{a}", [P, GT, 2]) for a in range(U)]
        var = sb("var", [P, GT])
        rstd = [sb(f"rstd{a}", [P, GT]) for a in range(U)]
        minus_rstd = sb("minus_rstd", [P, GT])
        shift = [sb(f"shift{a}", [P, GT]) for a in range(U)]
        power = sb("power", [P, GT])
        xn = [sb(f"xn{h}", [P, GT, D]) for h in range(2)]
        xt_hi = [sb(f"xt_hi{h}", [P, 2, GR], F32R) for h in range(2)]
        xt_lo = [sb(f"xt_lo{h}", [P, 2, GR], F32R) for h in range(2)]
        ident = constants["ident"]
        gate_w = constants["gate_w"]
        gate_b = constants["gate_b"]
        gate_parts = sb("r_gate_parts", [P, 2, 2, NEXP], F32R)
        lt = [sb(f"lt{h}", [2 * NEXP, GR]) for h in range(2)]
        logits = sb("logits", [P, NT, NEXP])
        logits_low = sb("logits_low", [P, NT, NEXP])
        valid = constants["valid"]
        tile_no = constants["tile_no"]
        row_no = constants["row_no"]
        falling = constants["falling"]
        thresholds = constants["thresholds"]
        before_f = constants["before"]
        before = sb("before", [P, P], BF16)
        ones = sb("ones", [P, P], BF16)
        ones_row = constants["ones_row"]
        iota = constants["iota"]
        best = sb("best", [P, NT])
        score = sb("score", [P, NT, NEXP])
        score2 = sb("score2", [P, NT, NEXP])
        first = sb("first", [P, NT])
        chosen = sb("chosen", [P, NEXP, NT], BF16)
        total = sb("total", [P, NEXP, NT])
        upto = sb("upto", [P, NEXP, NT])
        place = sb("place", [P, NEXP, NT])
        rank = sb("rank", [P, NT])
        rank_i = sb("rank_i", [P, NT], I32)
        high_i = sb("high_i", [P, NT], I32)
        low_i = sb("low_i", [P, NT], I32)
        high = sb("high", [P, NT])
        low = sb("low", [P, NT])
        upto_end = sb("upto_end", [P, NEXP])
        more = sb("more", [P, NEXP, EB])
        blocks_sum = sb("blocks_sum", [P, NEXP])
        blocks = sb("blocks", [P, NEXP])
        last_block = sb("last_block", [P, NEXP])
        begin = sb("begin", [P, NEXP])
        begin_tile = sb("begin_tile", [P, NT])
        kept = sb("kept", [P, NT])
        slot_tile = sb("slot_tile", [P, NT])
        slot_row = sb("slot_row", [P, NT])
        token_no = sb("token_no", [P, NT])
        in_row = sb("in_row", [P, V, P])
        in_tile = sb("in_tile", [P, V, NST])
        slot_now = sb("slot_now", [P, V])
        token_now = sb("token_now", [P, V])
        token = sb("token", [P, NST])
        empty = sb("empty", [P, NST])

        zeros = sb("zeros", [P, NST])
        banks = ps("banks", [P, 8, 512])
        ps_t = [banks[:, 2 * h:2 * h + 2] for h in range(2)]
        ps_l = [banks[:, 4 + h] for h in range(2)]
        ps_lt = [banks[:2 * NEXP, 6 + h] for h in range(2)]
        ps_place = banks[:, 0:3].rearrange("p b c -> p (b c)")
        ps_total = banks[:, 3:6].rearrange("p b c -> p (b c)")
        ps_table = banks[:, 6]

        rows_in = [sem(f"rows_in{a}") for a in range(U)]
        step_dve = sem("step_dve")
        spare_dve = sem("spare_dve")
        step_pool = sem("step_pool")
        spare_pool = sem("spare_pool")
        spare_pe = sem("spare_pe")
        mv_ready = sem("mv_ready")
        coef_ready = sem("r_coef_ready")
        xn_ready = sem("xn_ready")
        turned = sem("turned")
        gate_ready = sem("r_gate_ready")
        lt_ready = sem("lt_ready")
        lt_taken = sem("lt_taken")
        xt_act = sem("xt_act")
        xt_dve = sem("xt_dve")
        logits_ready = sem("logits_ready")
        logits_taken = sem("logits_taken")
        chosen_ready = sem("chosen_ready")
        before_ready = sem("before_ready")
        ones_ready = sem("ones_ready")
        total_ready = sem("total_ready")
        slots_ready = sem("slots_ready")
        pool_row_ready = sem("pool_row_ready")
        dve_row_ready = sem("dve_row_ready")
        in_tile_ready = sem("in_tile_ready")
        table_step = sem("table_step")

        x1_v = x1[:ROWS].rearrange("(g t p) c -> g p t c", t=GT, p=P)
        KC = NG // U

        block = ctx.enter_context(nc.Block())

        @block.sync
        def _(sp):
            for a in range(0, U, 2):
                sp.dma_start(rows[:, a], x1_v[a]).then_inc(rows_in[a], 16)
            def step(k):
                for a in range(U):
                    sp.wait_ge(xn_ready, U * k + (a + 1))
                    sp.dma_start(rows[:, a], x1_v[U * k + (U + a)]).then_inc(rows_in[a], 16)

            weights.load(sp, 0)
            weights.load_b2(sp)
            with sp.Fori(0, KC - 1) as k:
                step(k)
            sp.wait_ge(weights.hi_ready, 1)
            sp.wait_ge(weights.lo_ready, 1)
            weights.load(sp, 1)
            sp.wait_ge(weights.b2_in, 16)

        @block.gpsimd
        def _(pool):
            chain = Chain(pool, step_pool, spare_pool)

            def coefs(g, a):
                pool.wait_ge(mv_ready, g + 1)
                chain.apart()
                chain.link(nc.gpsimd.tensor_scalar(var[:], mv[a][:, :, 1], EPS, None, ALU.add))
                chain.link(nc.gpsimd.tensor_tensor(rstd[a][:], var[:], power[:], ALU.pow))
                chain.link(nc.gpsimd.tensor_scalar(minus_rstd[:], rstd[a][:], -1.0, None, ALU.mult))
                nc.gpsimd.tensor_tensor(shift[a][:], mv[a][:, :, 0], minus_rstd[:],
                                        ALU.mult).then_inc(coef_ready, 1)

            chain.link(nc.gpsimd.memset(power[:], -0.5))
            nc.gpsimd.memset(ones[:], 1.0).then_inc(ones_ready, 1)
            with pool.Fori(0, KC) as k:
                for a in range(U):
                    chain.enter(1 + (U * k + a) * 3)
                    coefs(U * k + a, a)
                    assert chain.n == 3
            weights.split_low(pool, nc, 0, 0)
            pool.wait_ge(slots_ready, 1)
            pool.sem_inc(pool_row_ready, 1)
            with pool.Fori(0, NT // V) as k:
                chain.enter(1 + 3 * NG + 2 * k)
                pool.wait_ge(pool_row_ready, len(POOL) * k + 1)
                chain.mark(nc.gpsimd.tensor_copy(slot_now[:], slot_row[:, bass.ds(V * k, V)]))
                chain.link(nc.gpsimd.tensor_copy(token_now[:], token_no[:, bass.ds(V * k, V)]))
                for a in POOL:
                    pool.wait_ge(table_step, V * k + (a + 1))
                    chain.apart()
                    nc.gpsimd.tensor_scalar(in_row[:, a], iota[:, :P], slot_now[:, a:a + 1],
                                            token_now[:, a:a + 1], ALU.is_equal,
                                            ALU.mult).then_inc(pool_row_ready, 1)

        @block.scalar
        def _(act):
            def normalise(g, a):
                act.wait_ge(coef_ready, g + 1)
                for t in range(GT):
                    ins = nc.scalar.activation(xn[a % 2][:, t], rows[:, a, t], ACT.Identity,
                                               bias=shift[a][:, t:t + 1], scale=rstd[a][:, t:t + 1])
                ins.then_inc(xn_ready, 1)

            def turned_rows(g, h):
                act.wait_ge(turned, g + 1)
                nc.scalar.copy(xt_hi[h][:], ps_t[h]).then_inc(xt_act, 1)

            def by_expert(g, h):
                act.wait_ge(lt_ready, g + 1)
                nc.scalar.copy(lt[h][:], ps_lt[h]).then_inc(lt_taken, 1)

            def step(g, a, last=NG):
                if last > 1:
                    turned_rows(g + 1, (a + 1) % 2)
                by_expert(g, a % 2)
                if last > 3:
                    normalise(g + 3, (a + 3) % U)

            for a in range(1, U, 2):
                act.dma_start(rows[:, a], x1_v[a]).then_inc(rows_in[a], 16)
            act.sem_inc(lt_taken, 1)
            normalise(0, 0)
            normalise(1, 1)
            turned_rows(0, 0)
            normalise(2, 2)
            step(0, 0)
            with act.Fori(0, KC - 1) as k:
                for a in range(U):
                    step(U * k + (a + 1), (a + 1) % U)
            for g in range(NG - U + 1, NG):
                step(g, g % U, NG - g)
            weights.split_high(nc, act, 0, 0)
            act.wait_ge(before_ready, 1)
            nc.scalar.copy(total[:].rearrange("p e t -> p (e t)"), ps_total[:, :NEXP * NT]).then_inc(total_ready, 1)

        @block.tensor
        def _(pe):

            def turn(g, h):
                pe.wait_ge(xn_ready, g + 1)
                for c in range(2):
                    for t in range(GT):
                        ins = nc.tensor.transpose(ps_t[h][:, c, t * P:(t + 1) * P],
                                                  xn[h][:, t, c * P:(c + 1) * P], ident[:])
                ins.then_inc(turned, 1)

            def gate(g, h):
                pe.wait_ge(xt_act, g + 1)
                pe.wait_ge(xt_dve, g + 1)
                for c in range(2):
                    nc.tensor.matmul(ps_lt[h], gate_parts[:, c].rearrange("p h e -> p (h e)"),
                                     xt_hi[h][:, c], start=c == 0, stop=False)
                for c in range(2):
                    ins = nc.tensor.matmul(ps_lt[h][:NEXP], gate_parts[:, c, 0], xt_lo[h][:, c],
                                           start=False, stop=c == 1)
                ins.then_inc(lt_ready, 1)

            def turn_back(g, h):
                pe.wait_ge(lt_taken, g + 2)
                pe.wait_ge(logits_taken, g + 1)
                pe.sem_inc(spare_pe, 1)
                for t in range(GT):
                    ins = nc.tensor.transpose(ps_l[h][:, 2 * NEXP * t:2 * NEXP * (t + 1)],
                                              lt[h][:, t * P:(t + 1) * P], ident[:2 * NEXP, :2 * NEXP])
                ins.then_inc(logits_ready, 1)

            def step(g, a, last=NG):
                if last > 1:
                    pe.wait_ge(xt_act, g)
                    pe.wait_ge(xt_dve, g)
                    turn(g + 1, (a + 1) % 2)
                pe.wait_ge(lt_taken, g)
                gate(g, a % 2)
                turn_back(g - 1, (a + 1) % 2)

            pe.wait_ge(gate_ready, 1)
            turn(0, 0)
            turn(1, 1)
            gate(0, 0)
            with pe.Fori(0, KC - 1) as k:
                for a in range(U):
                    step(U * k + (a + 1), (a + 1) % U)
            for g in range(NG - U + 1, NG):
                step(g, g % U, NG - g)
            turn_back(NG - 1, (NG - 1) % 2)
            pe.wait_ge(ones_ready, 1)
            pe.wait_ge(chosen_ready, 1)
            flat = chosen[:].rearrange("p e t -> p (e t)")
            for weights, dest in ((before, ps_place), (ones, ps_total)):
                for c in range(0, NEXP * NT, 512):
                    w = min(512, NEXP * NT - c)
                    ins = nc.tensor.matmul(dest[:, c:c + w], weights[:], flat[:, c:c + w],
                                           start=True, stop=True)
            ins.then_inc(before_ready, 1)
            nc.tensor.matmul(ps_table[:, :NST], zeros[:, :P], zeros[:], start=True,
                             stop=False).then_inc(table_step, V)
            with pe.Fori(0, NT // V) as k:
                for a in range(V):
                    if a in POOL:
                        pe.wait_ge(pool_row_ready, len(POOL) * k + (POOL.index(a) + 2))
                    else:
                        pe.wait_ge(dve_row_ready, len(DVE) * k + (DVE.index(a) + 1))
                    pe.wait_ge(in_tile_ready, V * k + (a + 1))
                    nc.tensor.matmul(ps_table[:, :NST], in_row[:, a], in_tile[:, a], start=False,
                                     stop=False).then_inc(table_step, 1)
            nc.tensor.matmul(ps_table[:, :NST], zeros[:, :P], zeros[:], start=False,
                             stop=True).then_inc(table_step, 1)

        @block.vector
        def _(v):
            chain = Chain(v, step_dve, spare_dve)
            tt, ts, stt, red = (nc.vector.tensor_tensor, nc.vector.tensor_scalar,
                                nc.vector.scalar_tensor_tensor, nc.vector.tensor_reduce)

            def statistics(g, k, a):
                v.wait_ge(rows_in[a], 16 * k + 16)
                for t in range(GT):
                    ins = nc.vector.bn_stats(stats[a % 2][:, t], rows[:, a, t])
                chain.link(ins)
                for t in range(GT):
                    ins = nc.vector.bn_aggr(mv[a][:, t], stats[a % 2][:, t])
                ins.then_inc(mv_ready, 1)

            def turned_half(g, h):
                v.wait_ge(turned, g + 1)
                v.wait_ge(xt_act, g + 1)
                tt(xt_lo[h][:], ps_t[h], xt_hi[h][:].bitcast(F32), ALU.subtract).then_inc(xt_dve, 1)

            def take(g, h):
                v.wait_ge(logits_ready, g + 1)
                parts = ps_l[h][:, :2 * GT * NEXP].rearrange("p (t h e) -> p t h e", h=2, e=NEXP)
                tt(logits[:, bass.ds(GT * g, GT), :], parts[:, :, 0],
                   gate_b[:].unsqueeze(1).broadcast_to([P, GT, NEXP]), ALU.add)
                nc.vector.tensor_copy(logits_low[:, bass.ds(GT * g, GT), :], parts[:, :, 1]).then_inc(logits_taken, 1)

            nc.vector.tensor_copy(before[:], before_f[:])
            chain.link(nc.vector.tensor_copy(gate_parts[:, :, 0], gate_w[:]))
            tt(gate_parts[:, :, 1], gate_w[:], gate_parts[:, :, 0].bitcast(F32), ALU.subtract).then_inc(gate_ready, 1)
            nc.vector.tensor_scalar(token_no[:], tile_no[:], float(P), row_no[:], ALU.mult, ALU.add)
            nc.vector.memset(zeros[:], 0.0).then_inc(logits_taken, 2)
            for g in range(4):
                statistics(g, 0, g)
            turned_half(0, 0)
            statistics(4, 1, 0)
            turned_half(1, 1)
            first_n = chain.n

            with v.Fori(0, KC - 2) as k:
                for a in range(U):
                    g = U * k + (a + 1)
                    chain.enter(first_n + (U * k + a))
                    statistics(g + 4, k + 1 + (a + 1) // U, (a + 1) % U)
                    turned_half(g + 1, a % 2)
                    take(g - 1, a % 2)
                    assert chain.n == 1
            chain.enter(first_n + U * (KC - 2))
            for g in range(NG - 2 * U + 1, NG):
                if g < NG - 4:
                    statistics(g + 4, (g + 4) // U, (g + 4) % U)
                if g < NG - 1:
                    turned_half(g + 1, (g + 1) % 2)
                take(g - 1, (g - 1) % 2)
            take(NG - 1, (NG - 1) % 2)
            v.wait_ge(logits_taken, NG + 2)

            def over_experts(x):
                return x[:].unsqueeze(2).broadcast_to([P, NT, NEXP])

            def over_tokens(x):
                return x[:].unsqueeze(1).broadcast_to([P, NT, NEXP])

            chain.link(tt(logits[:], logits[:], logits_low[:], ALU.add))
            chain.link(red(best[:], logits[:], AX.X, ALU.max))
            chain.link(tt(score[:], logits[:], over_experts(best), ALU.is_equal))
            chain.link(tt(score2[:], score[:], over_tokens(falling), ALU.mult))
            chain.link(red(first[:], score2[:], AX.X, ALU.max))
            chain.link(tt(score[:], score2[:], over_experts(first), ALU.is_equal))
            tt(chosen[:].rearrange("p e t -> p t e"), score[:], over_experts(valid),
               ALU.mult).then_inc(chosen_ready, 1)
            v.wait_ge(total_ready, 1)
            for e in range(NEXP):
                ins = nc.vector.tensor_tensor_scan(upto[:, e], ones_row[:], total[:, e], 0.0, ALU.mult, ALU.add)
            chain.link(ins)
            chain.mark(nc.vector.tensor_copy(upto_end[:], upto[:, :, NT - 1]))
            chain.link(tt(place[:], upto[:], total[:], ALU.subtract))
            chain.link(tt(upto[:].rearrange("p e t -> p (e t)"), place[:].rearrange("p e t -> p (e t)"),
                          ps_place[:, :NEXP * NT], ALU.add))
            chain.link(tt(place[:], upto[:], chosen[:], ALU.mult))
            chain.link(red(rank[:], place[:].rearrange("p e t -> p t e"), AX.X, ALU.add))
            chain.link(tt(more[:], upto_end[:].unsqueeze(2).broadcast_to([P, NEXP, EB]),
                          thresholds[:].unsqueeze(1).broadcast_to([P, NEXP, EB]), ALU.is_gt))
            chain.link(red(blocks_sum[:], more[:], AX.X, ALU.add))
            chain.link(ts(blocks[:], blocks_sum[:], 2.0, None, ALU.max))
            chain.link(nc.vector.tensor_tensor_scan(last_block[:], ones_row[:, :NEXP], blocks[:], 0.0,
                                                    ALU.mult, ALU.add))
            chain.mark(nc.vector.tensor_copy(first_block[:, 1:], last_block[:1]))
            chain.mark(nc.vector.memset(first_block[:, :1], 0))
            chain.link(tt(begin[:], last_block[:], blocks[:], ALU.subtract))
            chain.link(tt(score2[:], chosen[:].rearrange("p e t -> p t e"), over_tokens(begin), ALU.mult))
            chain.link(red(begin_tile[:], score2[:], AX.X, ALU.add))
            chain.mark(nc.vector.tensor_copy(rank_i[:], rank[:]))
            chain.mark(stt(out=kept[:], in0=rank[:], scalar=float(CAP), in1=valid[:], op0=ALU.is_lt, op1=ALU.mult))
            chain.wait()
            chain.mark(ts(high_i[:], rank_i[:], 7, None, ALU.logical_shift_right))
            chain.mark(ts(low_i[:], rank_i[:], 127, None, ALU.bitwise_and))
            chain.wait()
            chain.mark(nc.vector.tensor_copy(high[:], high_i[:]))
            chain.mark(nc.vector.tensor_copy(low[:], low_i[:]))
            chain.wait()
            stt(out=slot_tile[:], in0=begin_tile[:], scalar=float(BT), in1=high[:], op0=ALU.mult, op1=ALU.add)
            chain.link(stt(out=slot_row[:], in0=kept[:], scalar=-1000.0, in1=low[:], op0=ALU.mult, op1=ALU.add))
            ts(slot_row[:], slot_row[:], 1000.0, None, ALU.add).then_inc(slots_ready, 1)
            v.wait_ge(slots_ready, 1)

            with v.Fori(0, NT // V) as k:
                for a in range(V):
                    v.wait_ge(table_step, V * k + (a + 1))
                    t = bass.ds(V * k + a, 1)
                    if a in DVE:
                        ts(in_row[:, a], iota[:, :P], slot_row[:, t], token_no[:, t], ALU.is_equal,
                           ALU.mult).then_inc(dve_row_ready, 1)
                    ts(in_tile[:, a], iota[:, :NST], slot_tile[:, t], None,
                       ALU.is_equal).then_inc(in_tile_ready, 1)
            v.wait_ge(table_step, V + NT + 1)
            chain.link(nc.vector.tensor_copy(token[:], ps_table[:, :NST]))
            chain.mark(ts(empty[:], token[:], 0.0, float(ROWS), ALU.is_equal, ALU.mult))
            chain.mark(nc.vector.memset(take_row[:], ROWS - 1))
            chain.mark(nc.vector.memset(put_row[:], 1 << 17))
            chain.wait()
            chain.mark(stt(out=take_row[:, :NST], in0=token[:], scalar=-1.0, in1=empty[:], op0=ALU.add, op1=ALU.add))
            chain.link(ts(empty[:], empty[:], 8.0, None, ALU.mult))
            chain.link(stt(out=put_row[:, BT:], in0=token[:], scalar=-1.0, in1=empty[:], op0=ALU.add, op1=ALU.add))


class Weights:

    W1 = 2 * HID
    COLS = W1 + HID // P * D

    def __init__(self, ctx, nc, io):
        def sb(name, dt):
            return ctx.enter_context(nc.sbuf_tensor(name, [P, self.COLS], dt))

        self.raw = sb("w_raw", F32)
        self.hi = [sb(f"w_hi{s}", F32R) for s in range(2)]
        self.lo = [sb(f"w_lo{s}", F32R) for s in range(2)]
        self.raw_in = [ctx.enter_context(nc.semaphore(f"raw_in{n}")) for n in range(2)]
        self.hi_ready = ctx.enter_context(nc.semaphore("hi_ready"))
        self.lo_ready = ctx.enter_context(nc.semaphore("lo_ready"))
        self.spare = ctx.enter_context(nc.semaphore("w_spare"))
        self.b2 = ctx.enter_context(nc.sbuf_tensor("b2", [P, NEXP, D], F32))
        self.b2_row = io["b2"]
        self.b2_in = ctx.enter_context(nc.semaphore("b2_in"))
        self.w1 = io["w1"].rearrange("e (k p) f -> e p k f", p=P)
        self.w2 = io["w2"].rearrange("e (f p) c -> e p f c", p=P)

    def load_b2(self, sp):
        sp.dma_start(self.b2[:].rearrange("p e c -> p (e c)"),
                     self.b2_row.broadcast_to([P, NEXP * D])).then_inc(self.b2_in, 16)

    def load(self, sp, e):
        sp.dma_start(self.raw[:, :self.W1].rearrange("p (k f) -> p k f", k=2),
                     self.w1[e]).then_inc(self.raw_in[0], 16)
        sp.dma_start(self.raw[:, self.W1:].rearrange("p (f c) -> p f c", c=D),
                     self.w2[e]).then_inc(self.raw_in[1], 16)

    def split_high(self, nc, act, e, s):
        for n in range(2):
            act.wait_ge(self.raw_in[n], 16 * e + 16)
        nc.scalar.copy(self.hi[s][:], self.raw[:]).then_inc(self.hi_ready, 1)

    def split_low(self, pool, nc, e, s):
        for n in range(2):
            pool.wait_ge(self.raw_in[n], 16 * e + 16)
        pool.wait_ge(self.hi_ready, e + 1)
        pool.sem_inc(self.spare, 1)
        nc.gpsimd.tensor_tensor(self.lo[s][:], self.raw[:], self.hi[s][:].bitcast(F32),
                                ALU.subtract).then_inc(self.lo_ready, 1)


def expert_block(nc, io, out, take_row, put_row, first_block, weights, constants):
    KF = HID // P
    HB = BR // 2
    W1 = weights.W1
    with ExitStack() as ctx:
        def sb(name, shape, dt=F32):
            return ctx.enter_context(nc.sbuf_tensor(name, shape, dt))

        def ps(name, shape, dt=F32):
            return ctx.enter_context(nc.psum_tensor(name, shape, dt))

        def sem(name):
            return ctx.enter_context(nc.semaphore(name))

        w_hi, w_lo = weights.hi, weights.lo
        hi_ready, lo_ready = weights.hi_ready, weights.lo_ready
        b1, b2, ident = constants["b1"], weights.b2, constants["ident"]
        power = sb("f_power", [P, BT])
        gate_parts = sb("gate_parts", [P, 2, 2, NEXP], F32R)
        gate_b = constants["gate_b"]
        take_now = sb("take_now", [P, BT], I32)
        put_now = sb("put_now", [P, BT], I32)
        xg = sb("xg", [P, BT, D])
        stats = sb("f_stats", [P, BT, 6])
        mv = sb("f_mv", [P, BT, 2])
        var = sb("f_var", [P, BT])
        rstd = sb("f_rstd", [P, BT])
        minus_rstd = sb("f_minus_rstd", [P, BT])
        shift = sb("f_shift", [P, BT])
        xn = sb("f_xn", [P, BT, D])
        resid = sb("resid", [P, 3, BT, D])
        x_hi = sb("x_hi", [P, 2, BR], F32R)
        x_lo = sb("x_lo", [P, 2, BR], F32R)
        h_all = [sb(f"h_all{h}", [P, BR]) for h in range(2)]
        h_hi = sb("h_hi", [P, KF, BR], F32R)
        h_lo = sb("h_lo", [P, KF, BR], F32R)
        logit_parts = sb("logit_parts", [P, BT, 2 * NEXP])
        logits_sum = sb("logits_sum", [P, BT, NEXP])
        logits = sb("f_logits", [P, BT, NEXP])
        top = sb("top", [P, BT])
        below = sb("below", [P, BT, NEXP])
        power_e = sb("power_e", [P, BT, NEXP])
        total = sb("f_total", [P, BT])
        prob = sb("prob", [P, BT])
        y_sum = sb("y_sum", [P, 2, D])
        y_all = sb("y_all", [P, BT, D])
        finite = sb("finite", [P, BT, D], I32)
        negative = sb("negative", [P, BT, D])
        clean = sb("clean", [P, BT, D])
        y_out = sb("y_out", [P, BT, D])

        ps_h = ps("f_ps_h", [P, 2, 2, 512])
        ps_y = ps("f_ps_y", [P, 2, 512])
        ps_x = ps("f_ps_x", [P, 2, 512])

        gathered = sem("f_gathered")
        written = sem("written")
        step_dve = sem("f_step_dve")
        spare_dve = sem("f_spare_dve")
        spare_act = sem("f_spare_act")
        step_pool = sem("f_step_pool")
        spare_pool = sem("f_spare_pool")
        gate_ready = sem("gate_ready")
        mv_ready = sem("f_mv_ready")
        coef_ready = sem("f_coef_ready")
        xn_ready = sem("f_xn_ready")
        resid_ready = sem("resid_ready")
        turned = sem("f_turned")
        x_hi_ready = sem("x_hi_ready")
        x_lo_ready = sem("x_lo_ready")
        logits_ready = sem("f_logits_ready")
        logits_taken = sem("f_logits_taken")
        below_ready = sem("below_ready")
        exp_ready = sem("exp_ready")
        prob_ready = sem("prob_ready")
        cleared = sem("cleared")
        h_ready = sem("h_ready")
        h_all_ready = sem("h_all_ready")
        h_hi_ready = sem("h_hi_ready")
        h_lo_ready = sem("h_lo_ready")
        y_ready = sem("f_y_ready")
        y_sum_ready = sem("y_sum_ready")
        y_all_ready = sem("y_all_ready")
        clean_ready = sem("clean_ready")
        done_ready = sem("done_ready")
        finite_ready = sem("finite_ready")


        def bounds(engine, e):
            return (engine.value_load(first_block[0:1, bass.ds(e, 1)], min_val=0, max_val=NB - 2),
                    engine.value_load(first_block[0:1, bass.ds(e + 1, 1)], min_val=2, max_val=NB))

        block = ctx.enter_context(nc.Block())

        @block.sync
        def _(sp):
            with sp.Fori(0, NEXP - 2) as e:
                sp.wait_ge(hi_ready, e + 2)
                sp.wait_ge(lo_ready, e + 2)
                weights.load(sp, e + 2)
            sp.wait_ge(hi_ready, NEXP)
            sp.wait_ge(lo_ready, NEXP)
            weights.load(sp, NEXP - 1)
            for n in range(2):
                sp.wait_ge(weights.raw_in[n], 16 * (NEXP + 1))

        @block.gpsimd
        def _(pool):
            chain = Chain(pool, step_pool, spare_pool)

            def gather(b):
                chain.link(nc.gpsimd.tensor_copy(take_now[:], take_row[:, bass.ds(BT * b, BT)]))
                for i in range(BT):
                    nc.gpsimd.indirect_dma_start(
                        xg[:, i, :], None, out,
                        bass.IndirectOffsetOnAxis(take_now[:, i:i + 1].bitcast(U32), 0),
                        bounds_check=ROWS - 1).then_inc(gathered, 16)

            def coefs(b):
                pool.wait_ge(mv_ready, b + 1)
                chain.apart()
                chain.link(nc.gpsimd.tensor_scalar(var[:], mv[:, :, 1], EPS, None, ALU.add))
                chain.link(nc.gpsimd.tensor_tensor(rstd[:], var[:], power[:], ALU.pow))
                chain.link(nc.gpsimd.tensor_scalar(minus_rstd[:], rstd[:], -1.0, None, ALU.mult))
                nc.gpsimd.tensor_tensor(shift[:], mv[:, :, 0], minus_rstd[:], ALU.mult).then_inc(coef_ready, 1)

            def find_finite(b):
                pool.wait_ge(y_all_ready, BT * b + 1)
                chain.apart()
                nc.gpsimd.tensor_scalar(finite[:], y_all[:], 0.0, 0.0, ALU.mult,
                                        ALU.is_equal).then_inc(finite_ready, 1)

            def write(b):
                pool.wait_ge(clean_ready, b + 1)
                pool.wait_ge(written, 80 * b + 16)
                chain.apart()
                chain.mark(nc.gpsimd.tensor_copy(put_now[:], put_row[:, bass.ds(BT * b, BT)]))
                nc.gpsimd.tensor_tensor(y_out[:].unsqueeze(1), clean[:].unsqueeze(1),
                                        resid[:, bass.ds((b + 2) % 3, 1)], ALU.add).then_inc(done_ready, 1)
                pool.wait_ge(done_ready, b + 2)
                chain.wait()
                chain.apart()
                for i in range(BT):
                    nc.gpsimd.indirect_dma_start(
                        out, bass.IndirectOffsetOnAxis(put_now[:, i:i + 1].bitcast(U32), 0),
                        y_out[:, i, :], None, bounds_check=ROWS - 1, oob_is_err=False,
                    ).then_inc(written, 16)

            gather(0)
            chain.link(nc.gpsimd.memset(power[:], -0.5))
            chain.mark(nc.gpsimd.memset(resid[:, 2], 0.0))
            chain.mark(nc.gpsimd.memset(y_out[:], 0.0))
            chain.link(nc.gpsimd.memset(y_all[:], 0.0))
            pool.sem_inc(cleared, 1)
            pool.dma_start(io["spare"], y_out[:, 0, :]).then_inc(written, 16)
            pool.sem_inc(done_ready, 1)
            coefs(0)
            pool.wait_ge(resid_ready, 1)
            gather(1)
            coefs(1)
            first = chain.n
            PER = 1 + 1 + 3
            def step(b):
                chain.enter(first + PER * b)
                find_finite(b)
                pool.wait_ge(resid_ready, b + 2)
                pool.wait_ge(xn_ready, b + 2)
                chain.apart()
                gather(b + 2)
                write(b)
                coefs(b + 2)
                assert chain.n == PER, chain.n

            with pool.Fori(0, NEXP // 2) as pair:
                for s in range(2):
                    e = 2 * pair + s
                    start, end = bounds(pool, e)
                    step(start)
                    weights.split_low(pool, nc, e + 1, 1 - s)
                    with pool.Fori(start + 1, end) as b:
                        step(b)
            blocks = bounds(pool, NEXP - 1)[1]
            chain.enter(first + PER * blocks)
            find_finite(blocks)
            write(blocks)
            pool.wait_ge(written, 80 * blocks + 96)
            pool.wait_ge(gathered, 80 * blocks + 160)

        @block.scalar
        def _(act):
            def normalise(b, tiles):
                if 0 in tiles:
                    act.wait_ge(coef_ready, b + 1)
                    act.wait_ge(turned, BT * b + 1)
                for i in tiles:
                    ins = nc.scalar.activation(xn[:, i], xg[:, i], ACT.Identity,
                                               bias=shift[:, i:i + 1], scale=rstd[:, i:i + 1])
                if BT - 1 in tiles:
                    ins.then_inc(xn_ready, 1)

            def keep(b):
                act.wait_ge(done_ready, b)
                nc.scalar.copy(resid[:, bass.ds(b % 3, 1)], xg[:].unsqueeze(1)).then_inc(resid_ready, 1)

            def take_high(b, i):
                act.wait_ge(turned, BT * b + (i + 2))
                nc.scalar.copy(x_hi[:, :, i * P:(i + 1) * P],
                               ps_x[:, i % 2, :D].rearrange("p (k t) -> p k t", k=2)).then_inc(x_hi_ready, 1)

            act.sem_inc(h_all_ready, 2)
            act.wait_ge(cleared, 1)
            act.sem_inc(y_all_ready, 1)
            act.wait_ge(coef_ready, 1)
            for i in range(BT):
                ins = nc.scalar.activation(xn[:, i], xg[:, i], ACT.Identity,
                                           bias=shift[:, i:i + 1], scale=rstd[:, i:i + 1])
            ins.then_inc(xn_ready, 1)
            nc.scalar.copy(resid[:, 0], xg[:]).then_inc(resid_ready, 1)
            for i in range(BT):
                take_high(0, i)
            def step(e, b, split=None):
                for f in range(KF):
                    h = f % 2
                    act.wait_ge(h_ready, KF * b + (f + 1))
                    act.wait_ge(h_lo_ready, KF * b + (f + 1))
                    act.sem_inc(spare_act, 1)
                    nc.scalar.activation(h_all[h][:].rearrange("p (m t) -> p m t", m=2), ps_h[:, h, :, :HB],
                                         ACT.Relu, bias=b1[:, e, f:f + 1]).then_inc(h_all_ready, 1)
                    if f == 0:
                        act.wait_ge(below_ready, b + 1)
                        nc.scalar.activation(power_e[:], below[:], ACT.Exp).then_inc(exp_ready, 1)
                    if f < 3:
                        normalise(b + 1, range(2 * f, min(2 * f + 2, BT)))
                    if f == 3:
                        keep(b + 1)
                take_high(b + 1, 0)
                take_high(b + 1, 1)
                if split is not None:
                    weights.split_high(nc, act, e + 1, split)
                act.wait_ge(prob_ready, b + 1)
                act.wait_ge(clean_ready, b + 1)
                for i in range(BT):
                    act.wait_ge(y_sum_ready, BT * b + (i + 2))
                    nc.scalar.activation(y_all[:, i], y_sum[:, i % 2], ACT.Copy,
                                         scale=prob[:, i:i + 1]).then_inc(y_all_ready, 1)
                    if 1 <= i < BT - 1:
                        take_high(b + 1, i + 1)

            with act.Fori(0, NEXP // 2) as pair:
                for s in range(2):
                    e = 2 * pair + s
                    start, end = bounds(act, e)
                    step(e, start, 1 - s)
                    with act.Fori(start + 1, end) as b:
                        step(e, b)

        @block.tensor
        def _(pe):
            def turn(b, i):
                if i == 0:
                    pe.wait_ge(xn_ready, b + 1)
                pe.wait_ge(logits_taken, BT * b + (i + (i == 0)))
                for c in range(2):
                    ins = nc.tensor.transpose(ps_x[:, i % 2, c * P:(c + 1) * P], xn[:, i, c * P:(c + 1) * P],
                                              ident[:])
                ins.then_inc(turned, 1)

            def gate(b, i):
                pe.wait_ge(x_hi_ready, BT * b + (i + 1))
                pe.wait_ge(x_lo_ready, BT * b + (i + 1))
                tile = slice(i * P, (i + 1) * P)
                for c in range(2):
                    nc.tensor.matmul(ps_x[:, i % 2, D:D + 2 * NEXP], x_hi[:, c, tile],
                                     gate_parts[:, c].rearrange("p h e -> p (h e)"), start=c == 0, stop=False)
                for c in range(2):
                    ins = nc.tensor.matmul(ps_x[:, i % 2, D:D + NEXP], x_lo[:, c, tile],
                                           gate_parts[:, c, 0], start=False, stop=c == 1)
                ins.then_inc(logits_ready, 1)

            def up(b, s, f):
                h = f % 2
                pe.wait_ge(h_all_ready, KF * b + (f + 1))
                n = 0
                for c in range(2):
                    w = slice(c * HID + f * P, c * HID + (f + 1) * P)
                    for weights, x in ((w_hi, x_hi), (w_hi, x_lo), (w_lo, x_hi)):
                        for m in range(2):
                            ins = nc.tensor.matmul(ps_h[:, h, m, :HB], weights[s][:, w],
                                                   x[:, c, m * HB:(m + 1) * HB], start=n == 0, stop=n == 5)
                        n += 1
                ins.then_inc(h_ready, 1)

            def down(b, s, i):
                pe.wait_ge(y_sum_ready, BT * b + (i + (i == 0)))
                n = 0
                for f in range(KF):
                    if i == 0:
                        pe.wait_ge(h_hi_ready, KF * b + (f + 1))
                        pe.wait_ge(h_lo_ready, KF * b + (f + 3))
                    w = slice(W1 + f * D, W1 + (f + 1) * D)
                    for x, weights in ((h_hi, w_hi), (h_hi, w_lo), (h_lo, w_hi)):
                        ins = nc.tensor.matmul(ps_y[:, i % 2, :D], x[:, f, i * P:(i + 1) * P], weights[s][:, w],
                                               start=n == 0, stop=n == 3 * KF - 1)
                        n += 1
                ins.then_inc(y_ready, 1)

            pe.sem_inc(turned, 1)
            pe.wait_ge(gate_ready, 1)
            turn(0, 0)
            for i in range(1, BT):
                turn(0, i)
                gate(0, i - 1)
            gate(0, BT - 1)
            with pe.Fori(0, NEXP // 2) as pair:
                for s in range(2):
                    e = 2 * pair + s
                    start, end = bounds(pe, e)
                    with pe.Fori(start, end) as b:
                        pe.wait_ge(hi_ready, e + 1)
                        pe.wait_ge(lo_ready, e + 1)
                        for f in range(KF):
                            up(b, s, f)
                        turn(b + 1, 0)
                        turn(b + 1, 1)
                        for i in range(BT):
                            down(b, s, i)
                            gate(b + 1, i)
                            if 1 <= i < BT - 1:
                                turn(b + 1, i + 1)

        @block.vector
        def _(v):
            chain = Chain(v, step_dve, spare_dve)
            tt, ts, stt, red = (nc.vector.tensor_tensor, nc.vector.tensor_scalar,
                                nc.vector.scalar_tensor_tensor, nc.vector.tensor_reduce)

            def statistics(b):
                v.wait_ge(gathered, 80 * b + 80)
                for i in range(BT):
                    ins = nc.vector.bn_stats(stats[:, i], xg[:, i])
                chain.link(ins)
                for i in range(BT):
                    ins = nc.vector.bn_aggr(mv[:, i], stats[:, i])
                ins.then_inc(mv_ready, 1)

            def take_low(b, i):
                v.wait_ge(x_hi_ready, BT * b + (i + 1))
                tt(x_lo[:, :, i * P:(i + 1) * P], ps_x[:, i % 2, :D].rearrange("p (k t) -> p k t", k=2),
                   x_hi[:, :, i * P:(i + 1) * P].bitcast(F32), ALU.subtract).then_inc(x_lo_ready, 1)

            def take_logits(b, i):
                v.wait_ge(logits_ready, BT * b + (i + 1))
                nc.vector.tensor_copy(logit_parts[:, i], ps_x[:, i % 2, D:D + 2 * NEXP]).then_inc(logits_taken, 1)

            gate_2 = constants["gate_w"][:]
            chain.link(nc.vector.tensor_copy(gate_parts[:, :, 0], gate_2))
            tt(gate_parts[:, :, 1], gate_2, gate_parts[:, :, 0].bitcast(F32), ALU.subtract).then_inc(gate_ready, 1)
            v.sem_inc(y_sum_ready, 1)
            v.sem_inc(logits_taken, 1)
            v.sem_inc(h_lo_ready, 2)
            statistics(0)
            take_low(0, 0)
            for i in range(1, BT):
                take_low(0, i)
                take_logits(0, i - 1)
            take_logits(0, BT - 1)
            statistics(1)

            first = chain.n
            PER = 3 + 1 + 3 + 1

            def infinite_above(b):
                v.wait_ge(y_all_ready, BT * b + 1)
                v.wait_ge(done_ready, b + 1)
                chain.mark(ts(clean[:], y_all[:], LARGEST, 1e4, ALU.is_gt, ALU.mult))

            def infinite_below():
                chain.mark(ts(negative[:], y_all[:], -LARGEST, -1e4, ALU.is_lt, ALU.mult))

            def add_infinities():
                chain.wait()
                chain.link(tt(clean[:], clean[:], negative[:], ALU.add))

            def keep_finite(b):
                v.wait_ge(finite_ready, b + 1)
                chain.apart()
                nc.vector.copy_predicated(clean[:], finite[:], y_all[:]).then_inc(clean_ready, 1)

            with v.Fori(0, NEXP // 2) as pair:
                for s in range(2):
                    e = 2 * pair + s
                    start, end = bounds(v, e)
                    with v.Fori(start, end) as b:
                        chain.enter(first + PER * b)
                        v.wait_ge(logits_taken, BT * b + (BT + 1))
                        chain.link(tt(logits_sum[:], logit_parts[:, :, :NEXP], logit_parts[:, :, NEXP:], ALU.add))
                        chain.link(tt(logits[:], logits_sum[:], gate_b[:].unsqueeze(1).broadcast_to([P, BT, NEXP]),
                                      ALU.add))
                        chain.link(red(top[:], logits[:], AX.X, ALU.max))
                        tt(below[:], logits[:], top[:].unsqueeze(2).broadcast_to([P, BT, NEXP]),
                           ALU.subtract).then_inc(below_ready, 1)
                        for f in range(KF):
                            v.wait_ge(h_all_ready, KF * b + (f + 3))
                            nc.vector.tensor_copy(h_hi[:, f], h_all[f % 2][:]).then_inc(h_hi_ready, 1)
                            v.wait_ge(h_hi_ready, KF * b + (f + 1))
                            tt(h_lo[:, f], h_all[f % 2][:], h_hi[:, f].bitcast(F32),
                               ALU.subtract).then_inc(h_lo_ready, 1)
                            if f == 2:
                                v.wait_ge(exp_ready, b + 1)
                                v.wait_ge(y_all_ready, BT * b + 1)
                                chain.link(red(total[:], power_e[:], AX.X, ALU.add))
                                nc.vector.reciprocal(prob[:], total[:]).then_inc(prob_ready, 1)
                            if f == 3:
                                infinite_above(b)
                            if f == 4:
                                infinite_below()
                        take_low(b + 1, 0)
                        take_low(b + 1, 1)
                        add_infinities()
                        for i in range(BT):
                            v.wait_ge(y_ready, BT * b + (i + 1))
                            v.wait_ge(y_all_ready, BT * b + (i + (i == 0)))
                            tt(y_sum[:, i % 2], ps_y[:, i % 2, :D], b2[:, e], ALU.add).then_inc(y_sum_ready, 1)
                            take_logits(b + 1, i)
                            if 1 <= i < BT - 1:
                                take_low(b + 1, i + 1)
                            if i == 0:
                                keep_finite(b)
                            if i == 1:
                                statistics(b + 2)
                        assert chain.n == PER, chain.n
            blocks = bounds(v, NEXP - 1)[1]
            chain.enter(first + PER * blocks)
            infinite_above(blocks)
            infinite_below()
            add_infinities()
            keep_finite(blocks)




def build(nc, io, out):
    with ExitStack() as ctx:
        def table(name, shape):
            return ctx.enter_context(nc.sbuf_tensor(name, shape, I32))

        take_row = table("take_row", [P, NST + 2 * BT])
        put_row = table("put_row", [P, BT + NST])
        first_block = table("first_block", [1, NEXP + 1])
        constants = Constants(ctx, nc, io)
        edge_and_node_block(nc, io, out, constants)
        weights = Weights(ctx, nc, io)
        routing_block(nc, io, out, take_row, put_row, first_block, weights, constants)
        expert_block(nc, io, out, take_row, put_row, first_block, weights, constants)


def layout(x, src, dst, ea3, ea8, w):
    f = np.float32
    pad = EPAD - NE
    own = np.arange(GR)
    xp = np.concatenate([x, np.zeros((ROWS - NN, D), f)])
    srcp = np.concatenate([src, np.zeros(pad, np.int32)]).astype(np.int32)
    dstp = np.concatenate([dst, (ROWS + np.arange(NE, EPAD) % GR)]).astype(np.int32)
    ea3p = np.concatenate([ea3, np.zeros((pad, 3), f)])
    ea8p = np.concatenate([ea8, np.zeros((pad, 8), f)])
    lin = np.zeros((D, D), f)
    lin[:MUL, :MUL] = w["L0_gnn_lin_w0"]
    for i in range(3):
        lin[MUL + i::3, MUL + i::3] = w["L0_gnn_lin_w1"]
    t = np.arange(NT)
    p = np.arange(P)[:, None]
    return {
        "gate_w": w["L0_ffn_gate_w"].reshape(2, P, NEXP).transpose(1, 0, 2),
        "gate_b": np.broadcast_to(w["L0_ffn_gate_b"], (P, NEXP)),
        "w1": w["L0_ffn_w1"],
        "w2": w["L0_ffn_w2"],
        "b1": w["L0_ffn_b1"].reshape(NEXP, HID // P, P).transpose(2, 0, 1),
        "b2": w["L0_ffn_b2"].reshape(1, NEXP * D),
        "ident": np.eye(P, dtype=f),
        "valid": (t * P + p < NN).astype(f),
        "tile_no": np.broadcast_to(t, (P, NT)).astype(f),
        "row_no": (p + 1).astype(f),
        "falling": np.broadcast_to(NEXP - np.arange(NEXP), (P, NEXP)).astype(f),
        "thresholds": np.broadcast_to(BR * np.arange(EB), (P, EB)).astype(f),
        "before": (np.arange(P) > p).astype(f),
        "iota": np.broadcast_to(np.arange(256), (P, 256)).astype(f),
        "ones_row": np.ones((P, NT), f),
        "x": xp,
        "dst": dstp,
        "src_tiles": srcp.reshape(-1, P).T,
        "dst_tiles": dstp[:EG * GR].reshape(-1, P).T,
        "vec_tiles": ea3p.reshape(-1, P, 3).transpose(1, 0, 2),
        "emb": ea8p.reshape(-1, GR, 8).transpose(0, 2, 1),
        "trash": (ROWS + own).reshape(GT, P).T.astype(f),
        "upper": (own[None] >= np.arange(P)[:, None]).astype(f),
        "lin": lin.reshape(2, P, D).transpose(1, 0, 2),
        "fc1": w["L0_gnn_fc_w1"],
        "fc2": w["L0_gnn_fc_w2"],
    }


def kernel(x, src, dst, edge_attr_3, edge_attr_8, **w):
    import concourse.bacc as bacc
    from concourse.bass_utils import run_bass_kernel_spmd

    nc = bacc.Bacc("TRN2", target_bir_lowering=False, num_devices=1)
    w = {k: np.asarray(a) for k, a in w.items()}
    arrays = layout(*(np.asarray(a) for a in (x, src, dst, edge_attr_3, edge_attr_8)), w)
    arrays = {k: np.ascontiguousarray(a) for k, a in arrays.items()}
    io = {k: nc.dram_tensor(f"in_{k}", a.shape, mybir.dt.from_np(a.dtype), kind="ExternalInput").ap()
          for k, a in arrays.items()}
    out = nc.dram_tensor("out", (ROWS + GR, D), F32, kind="ExternalOutput").ap()
    io["spare"] = nc.dram_tensor("spare", (P, D), F32).ap()
    build(nc, io, out)
    r = run_bass_kernel_spmd(nc, [{f"in_{k}": a for k, a in arrays.items()}], core_ids=[0])
    return r.results[0]["out"][:NN]
```
